# Optimizing a Trainium2 kernel written in Bass

```python
import numpy as np
import jax
import jax.numpy as jnp

def _softmax(x, axis=-1):
    return jax.nn.softmax(x, axis=axis)

def _gelu(x):
    return jax.nn.gelu(x, approximate=True)

def _silu(x):
    return jax.nn.silu(x)

def _sigmoid(x):
    return jax.nn.sigmoid(x)

def _layernorm(x, axis=-1, eps=1e-05):
    m = jnp.mean(x, axis=axis, keepdims=True)
    v = jnp.var(x, axis=axis, keepdims=True)
    return (x - m) / jnp.sqrt(v + eps)

def _scatter_add(tgt, idx, src, axis=0):
    return tgt.at[idx].add(src)

def _segment_sum(src, seg, n):
    return jax.ops.segment_sum(src, seg, n)
kernel_name = 'mk_lm_tower_d1_tok_ids2048_r4_3226a8'

def setup_inputs(seed: int=0):
    np.random.seed(seed)
    _w = jnp.asarray

    def _rec_inputs():
        import jax
        import jax.numpy as jnp
        _rk = jax.random.key(seed)
        x = jax.random.randint(jax.random.fold_in(_rk, 1), (2, 2048), 0, 168, jnp.int32)
        return x
    x = _rec_inputs()

    def _L0_tok_setup():
        import jax, jax.numpy as jnp
        import numpy as np
        NUM_SLOTS = 168
        NUM_CATS = 512
        BATCH, SEQ = (128, 200)
        key = jax.random.key(seed)
        k1, k2 = jax.random.split(key)
        inputs_hour = jax.random.randint(k1, (BATCH, SEQ), 0, NUM_SLOTS)
        catid_time_matrix = jax.random.normal(k2, (NUM_SLOTS, NUM_CATS), dtype=jnp.float32)
        return {'inputs_hour': inputs_hour, 'catid_time_matrix': catid_time_matrix}
    _L0_tok_all = _L0_tok_setup()
    _L0_tok_in = {k: v for k, v in _L0_tok_all.items() if k in ('catid_time_matrix',)}
    del _L0_tok_all

    def _L0_attn_setup():
        import jax, jax.numpy as jnp
        import numpy as np
        D_MODEL = 512
        STATE = 16
        KCONV = 4
        EXPAND = 2
        D_INNER = D_MODEL * EXPAND
        EPS = 1e-05

        def _silu(v):
            return v * jax.nn.sigmoid(v)
        key = jax.random.key(seed)
        ks = jax.random.split(key, 10)
        s = 0.02
        x = jax.random.normal(ks[0], (2, 512, D_MODEL), dtype=jnp.float32)
        norm_w = jnp.ones((D_MODEL,), jnp.float32)
        in_proj_w = jax.random.normal(ks[1], (D_INNER * 2, D_MODEL), jnp.float32) * s
        conv_w = jax.random.normal(ks[2], (D_INNER, 1, KCONV), jnp.float32) * s
        conv_b = jnp.zeros((D_INNER,), jnp.float32)
        x_proj_w = jax.random.normal(ks[3], (STATE * 2 + 1, D_INNER), jnp.float32) * s
        dt_w = jax.random.normal(ks[4], (D_INNER, 1), jnp.float32) * s
        dt_b = jnp.zeros((D_INNER,), jnp.float32)
        A_log = jnp.log(jnp.broadcast_to(jnp.arange(1, STATE + 1, dtype=jnp.float32)[None, :], (D_INNER, STATE)))
        D_param = jnp.ones((D_INNER,), jnp.float32)
        out_proj_w = jax.random.normal(ks[5], (D_MODEL, D_INNER), jnp.float32) * s
        return {'x': x, 'norm_w': norm_w, 'in_proj_w': in_proj_w, 'conv_w': conv_w, 'conv_b': conv_b, 'x_proj_w': x_proj_w, 'dt_w': dt_w, 'dt_b': dt_b, 'A_log': A_log, 'D_param': D_param, 'out_proj_w': out_proj_w}
    _L0_attn_all = _L0_attn_setup()
    _L0_attn_in = {k: v for k, v in _L0_attn_all.items() if k in ('norm_w', 'in_proj_w', 'conv_w', 'conv_b', 'x_proj_w', 'dt_w', 'dt_b', 'A_log', 'D_param', 'out_proj_w')}
    del _L0_attn_all

    def _L0_ffn_setup():
        import jax, jax.numpy as jnp
        import numpy as np
        HIDDEN = 512
        INTER = 1376
        LUT_SIZE = 16

        def _ghost_linear(x, idx, lut):
            w = lut[idx]
            return jnp.einsum('bsh,oh->bso', x, w)
        key = jax.random.key(seed)
        k_x, k_lut, k_g, k_u, k_d = jax.random.split(key, 5)
        x = jax.random.normal(k_x, (2, 1024, HIDDEN), dtype=jnp.float32)
        lut = jax.random.normal(k_lut, (LUT_SIZE,), dtype=jnp.float32) * 0.02
        gate_idx = jax.random.randint(k_g, (INTER, HIDDEN), 0, LUT_SIZE, dtype=jnp.int32)
        up_idx = jax.random.randint(k_u, (INTER, HIDDEN), 0, LUT_SIZE, dtype=jnp.int32)
        down_idx = jax.random.randint(k_d, (HIDDEN, INTER), 0, LUT_SIZE, dtype=jnp.int32)
        return {'x': x, 'lut': lut, 'gate_idx': gate_idx, 'up_idx': up_idx, 'down_idx': down_idx}
    _L0_ffn_all = _L0_ffn_setup()
    _L0_ffn_in = {k: v for k, v in _L0_ffn_all.items() if k in ('lut', 'gate_idx', 'up_idx', 'down_idx')}
    del _L0_ffn_all
    return {'x': x, 'L0_tok_catid_time_matrix': _L0_tok_in['catid_time_matrix'], 'L0_attn_norm_w': _L0_attn_in['norm_w'], 'L0_attn_in_proj_w': _L0_attn_in['in_proj_w'], 'L0_attn_conv_w': _L0_attn_in['conv_w'], 'L0_attn_conv_b': _L0_attn_in['conv_b'], 'L0_attn_x_proj_w': _L0_attn_in['x_proj_w'], 'L0_attn_dt_w': _L0_attn_in['dt_w'], 'L0_attn_dt_b': _L0_attn_in['dt_b'], 'L0_attn_A_log': _L0_attn_in['A_log'], 'L0_attn_D_param': _L0_attn_in['D_param'], 'L0_attn_out_proj_w': _L0_attn_in['out_proj_w'], 'L0_ffn_lut': _L0_ffn_in['lut'], 'L0_ffn_gate_idx': _L0_ffn_in['gate_idx'], 'L0_ffn_up_idx': _L0_ffn_in['up_idx'], 'L0_ffn_down_idx': _L0_ffn_in['down_idx']}

def reference(x, L0_tok_catid_time_matrix, L0_attn_norm_w, L0_attn_in_proj_w, L0_attn_conv_w, L0_attn_conv_b, L0_attn_x_proj_w, L0_attn_dt_w, L0_attn_dt_b, L0_attn_A_log, L0_attn_D_param, L0_attn_out_proj_w, L0_ffn_lut, L0_ffn_gate_idx, L0_ffn_up_idx, L0_ffn_down_idx):
    import jax
    import jax.numpy as jnp

    def _L0_tok_ref(inputs_hour, catid_time_matrix):
        import jax, jax.numpy as jnp
        import numpy as np
        NUM_SLOTS = 168
        NUM_CATS = 512
        BATCH, SEQ = (128, 200)
        probs = jax.nn.softmax(catid_time_matrix, axis=1)
        return probs[inputs_hour]

    def _L0_attn_ref(x, norm_w, in_proj_w, conv_w, conv_b, x_proj_w, dt_w, dt_b, A_log, D_param, out_proj_w):
        import jax, jax.numpy as jnp
        import numpy as np
        D_MODEL = 512
        STATE = 16
        KCONV = 4
        EXPAND = 2
        D_INNER = D_MODEL * EXPAND
        EPS = 1e-05

        def _silu(v):
            return v * jax.nn.sigmoid(v)
        residual = x
        xn = x * jax.lax.rsqrt(jnp.mean(x * x, axis=-1, keepdims=True) + EPS) * norm_w
        xz = jnp.einsum('bld,ed->ble', xn, in_proj_w)
        x_inner, z = jnp.split(xz, 2, axis=-1)
        xc = jnp.transpose(x_inner, (0, 2, 1))
        xc = jax.lax.conv_general_dilated(xc, conv_w, window_strides=(1,), padding=[(KCONV - 1, 0)], dimension_numbers=('NCH', 'OIH', 'NCH'), feature_group_count=D_INNER)
        xc = xc + conv_b[None, :, None]
        xc = _silu(jnp.transpose(xc, (0, 2, 1)))
        x_ssm = jnp.einsum('bld,ed->ble', xc, x_proj_w)
        dt = jax.nn.softplus(x_ssm[..., -1:] * dt_w[:, 0] + dt_b)
        B_p = x_ssm[..., :STATE]
        C_p = x_ssm[..., STATE:2 * STATE]
        A = -jnp.exp(A_log)
        batch = x.shape[0]
        h0 = jnp.zeros((batch, D_INNER, STATE), x.dtype)

        def step(h, inp):
            dt_t, B_t, C_t, u_t = inp
            dA = jnp.exp(dt_t[..., None] * A)
            h = dA * h + (dt_t * u_t)[..., None] * B_t[:, None, :]
            y_t = jnp.sum(h * C_t[:, None, :], axis=-1) + D_param * u_t
            return (h, y_t)
        seq_first = lambda a: jnp.swapaxes(a, 0, 1)
        _, ys = jax.lax.scan(step, h0, (seq_first(dt), seq_first(B_p), seq_first(C_p), seq_first(xc)))
        y = jnp.swapaxes(ys, 0, 1)
        y = y * _silu(z)
        return jnp.einsum('ble,de->bld', y, out_proj_w) + residual

    def _L0_ffn_ref(x, lut, gate_idx, up_idx, down_idx):
        import jax, jax.numpy as jnp
        import numpy as np
        HIDDEN = 512
        INTER = 1376
        LUT_SIZE = 16

        def _ghost_linear(x, idx, lut):
            w = lut[idx]
            return jnp.einsum('bsh,oh->bso', x, w)
        gate = _ghost_linear(x, gate_idx, lut)
        up = _ghost_linear(x, up_idx, lut)
        h = jax.nn.silu(gate) * up
        return _ghost_linear(h, down_idx, lut)
    h = _L0_tok_ref(x, L0_tok_catid_time_matrix)
    h = h + _L0_attn_ref(_layernorm(h, axis=-1), L0_attn_norm_w, L0_attn_in_proj_w, L0_attn_conv_w, L0_attn_conv_b, L0_attn_x_proj_w, L0_attn_dt_w, L0_attn_dt_b, L0_attn_A_log, L0_attn_D_param, L0_attn_out_proj_w)
    h = h + _L0_ffn_ref(_layernorm(h, axis=-1), L0_ffn_lut, L0_ffn_gate_idx, L0_ffn_up_idx, L0_ffn_down_idx)
    return h

_drawn_inputs = setup_inputs


def setup_inputs(seed=0):
    import zlib

    import numpy as np

    out = dict(_drawn_inputs(seed))
    spreads = {'L0_attn_norm_w': (1.0, 0.6),
     'L0_attn_conv_b': (0.0, 0.578),
     'L0_attn_dt_b': (0.0, 0.8),
     'L0_attn_D_param': (1.0, 0.6)}
    factors = {'L0_attn_in_proj_w': 4.103,
     'L0_attn_conv_w': 8.0,
     'L0_attn_x_proj_w': 8.0,
     'L0_attn_dt_w': 8.0,
     'L0_attn_A_log': 8.0,
     'L0_attn_out_proj_w': 4.009,
     'L0_ffn_lut': 8.0}
    for name, (base, spread) in spreads.items():
        noise = np.random.default_rng([zlib.crc32(name.encode()), seed]).standard_normal(out[name].shape)
        drawn = base * np.exp(spread * noise) if base else spread * noise
        out[name] = jnp.asarray(drawn.astype(out[name].dtype))
    for name, factor in factors.items():
        out[name] = (out[name] * factor).astype(out[name].dtype)
    return out
```

```python
from contextlib import ExitStack

import concourse.bass as bass
from concourse import mybir

F32 = mybir.dt.float32
BF16 = mybir.dt.bfloat16
I32 = mybir.dt.int32
ALU = mybir.AluOpType
ACT = mybir.ActivationFunctionType
AX_X = mybir.AxisListType.X

P = 128
V = 168
V1 = V - P
DM = 512
DK = DM // P
DI = 1024
ET = DI // P
NS = 16
TOK = 4096
SEQ = 2048
LUTN = 16
FF = 1376
OT = (FF + P - 1) // P
WTILES = 3 * OT
EPS = 1e-5

TA = 512
HALO = 3
NA = TOK // TA
TB = 256
NB = TOK // TB
CPB = SEQ // TB
TBB = TB // P
QN = 4
GQ = NS // QN
QUADS = ET * GQ
PAIRS = ET // 2
QP = 2 * GQ
NG = 2
NF = 3
BIG = 3.4028e38

CB, CZ, CX = 0, DM, DM + DI
CT = DM + 2 * DI


def plan():
    pe = {s: [] for s in range(QUADS + 1)}
    act = {s: [] for s in range(QUADS + 1)}
    dve = {s: [] for s in range(QUADS + 1)}
    pool = {s: [] for s in range(QUADS + 1)}
    for tb in range(TBB):
        pe[2 * tb] += [("op", tb, 0)]
        pe[2 * tb + 1] += [("op", tb, 1)]
        act[2 * tb + 2] += [("h2", tb)]
        dve[2 * tb + 3] += [("stats", tb)]
        pool[2 * tb + 4] += [("rstd", tb)]
        dve[2 * tb + 5] += [("norm", tb)]
        pe[2 * tb + 6] += [("xt", tb)]
        act[2 * tb + 7] += [("xnT", tb)]
    dve[6] += [("onehot",)]
    for p in range(PAIRS):
        s = min(QP * p + QP + 1, QUADS)
        pe[s] += [("sz", p), ("yb", p)]
        act[min(QP * p + QP, QUADS)] += [("yT", p)]
        dve[min(s + 1, QUADS)] += [("fin", p)]
    for o, s in enumerate([10, 11, 12, 13, 15, 16, 18, 19, 20, 22, 23]):
        pe[s] += [("gu", o)]
        act[s + 1] += [("tanh", o)]
        dve[s + 2] += [("mid", o)]
    for tb in range(TBB):
        for j in range(3):
            pe[25 + 3 * tb + j] += [("dn", tb, j)]
        dve[28 + 3 * tb] += [("out", tb)]
        act[30 + 2 * tb] += [("store", tb)]
    return pe, act, dve, pool


PE_PLAN, ACT_PLAN, DVE_PLAN, POOL_PLAN = plan()
SCAN_ONLY = ("sz", "yb", "yT", "fin", "onehot")
LAST_PART = {"op": 1, "dn": 2}


def bank_uses(with_scan):
    seq = []
    for s in range(QUADS + 1):
        for t in PE_PLAN[s]:
            if not with_scan and t[0] in SCAN_ONLY:
                continue
            if t[:2] not in seq:
                seq.append(t[:2])
    return seq


USES = bank_uses(True)


class Banks:

    def __init__(self, with_scan):
        self.seq = bank_uses(with_scan)
        done = []
        for s in range(QUADS + 1):
            for t in PE_PLAN[s]:
                if t[:2] in self.seq and (t[0] not in LAST_PART or t[2] == LAST_PART[t[0]]):
                    done.append(t[:2])
        self.done = done

    def bank(self, use):
        return self.seq.index(use) % NF

    def filled(self, use):
        return self.done.index(use) + 1

    def previous(self, use):
        n = self.seq.index(use)
        if n >= NF:
            return self.seq[n - NF], False
        return [u for m, u in enumerate(USES) if m % NF == n % NF][-1], True


def lm_tower_kernel(nc, ids_a, ids_b, table, norm_w, in_wT, conv_w, conv_b, xp_wT, dt_w, dt_b, a_log,
                    d_par, out_wT, lut, widx, out):
    chan = nc.dram_tensor("chan", [P, ET, 3, TOK], F32, kind="Internal").ap()
    bc = nc.dram_tensor("bc", [2 * NS, TOK], F32, kind="Internal").ap()

    with ExitStack() as ctx:
        def sb(name, shape, dt):
            return ctx.enter_context(nc.sbuf_tensor(name, shape, dt))

        def sem(name):
            return ctx.enter_context(nc.semaphore(name))

        ffw = sb("ffw", [P, WTILES, DM], F32)
        outw = sb("outw", [P, ET, DM], F32)
        part = sb("part", [P, 3, CX], BF16)
        pack = sb("pack", [P, CX], BF16)
        a_neg = sb("a_neg", [P, ET * NS], F32)
        dpar = sb("dpar", [P, ET], F32)
        ident = sb("ident", [P, P], F32)
        rows = sb("rows", [P, 2], F32)
        eps_e = sb("eps_e", [P, 1], F32)
        state = sb("state", [P, ET * NS], F32)
        work = sb("work", [P, 28640], F32)
        psum = ctx.enter_context(nc.psum_tensor("psum", [P, 8, 512], F32))

        class Region:

            def __init__(self, at=0):
                self.at = at

            def cut(self, shape, dt=F32):
                n = 1
                for d in shape:
                    n *= d
                words = (n * (2 if dt == BF16 else 4) + 3) // 4
                assert self.at + words <= 28640, self.at + words
                v = work[:, self.at:self.at + words]
                self.at += words
                if dt != F32:
                    v = v.bitcast(dt)
                    v = v[:, 0:n]
                if len(shape) == 2:
                    v = v.rearrange("p (a b) -> p a b", b=shape[1])
                elif len(shape) == 3:
                    v = v.rearrange("p (a b c) -> p a b c", b=shape[1], c=shape[2])
                return v

        ra = Region()
        u_sb = [ra.cut([ET, TA]) for _ in range(2)]
        soft = ra.cut([ET, TA])
        relu = ra.cut([ET, TA])
        xpart = ra.cut([3, DI], BF16)
        xpack = ra.cut([DI], BF16)
        xpw = ra.cut([ET, 2 * NS + 1])
        xdtw = ra.cut([ET, P])
        idsa = [ra.cut([TA + HALO], I32) for _ in range(2)]
        stage_a_buffers = ra.at
        oha = [ra.cut([2, TA + HALO + 1], BF16) for _ in range(2)]
        acc = [ra.cut([TA]) for _ in range(2)]
        pre = [ra.cut([TA]) for _ in range(2)]
        bcs = [ra.cut([TA]) for _ in range(2)]
        widx_sb = [ra.cut([DM], I32) for _ in range(2)]
        prod = [ra.cut([DM]) for _ in range(4)]
        assert ra.at - stage_a_buffers >= 1024 + DK * V + 1024 + 3 * CT // 2 + 32
        lut_sb = ra.cut([LUTN])
        cw = ra.cut([ET, 4])
        cb = ra.cut([ET])
        dtw = ra.cut([ET])
        dtb = ra.cut([ET])
        nw = ra.cut([DK])
        row_i = ra.cut([2], I32)
        rt = Region()
        inw = rt.cut([DK, 2 * DI])
        full = rt.cut([2, CT])
        rest = rt.cut([CT])
        rs2 = Region(stage_a_buffers)
        tab = rs2.cut([2, DM])
        xnt = rs2.cut([DK, V])
        tmp = rs2.cut([2, DM])
        lo_st = rs2.cut([3, CT], BF16)
        stt = rs2.cut([2, 16])

        rb = Region()
        b_rep = rb.cut([NS, TB])
        c_rep = rb.cut([NS, TB])
        tiles = [rb.cut([2, 3, TB]) for _ in range(2)]
        dbu = [rb.cut([QN, TB]) for _ in range(2)]
        hc = [rb.cut([QN, TB]) for _ in range(NG)]
        yts = rb.cut([2, TBB * P])
        ysum = rb.cut([2, TB])
        yg = rb.cut([ET, TB])
        h2 = rb.cut([TBB, DM])
        xn2 = rb.cut([TBB, DM])
        xn2t = rb.cut([DK, TB])
        mid = rb.cut([OT, TB])
        th = [rb.cut([TB]) for _ in range(2)]
        sg = rb.cut([TB])
        osb = rb.cut([TBB, DM])
        ohb = rb.cut([2, TB], BF16)
        idsb = rb.cut([TB], I32)
        st2 = rb.cut([TBB, 16])

        s_const = sem("constants_built")
        s_w = sem("small_weights_loaded")
        s_in = sem("in_proj_loaded")
        s_outw = sem("out_proj_loaded")
        s_tab = sem("table_loaded")
        v_tab = sem("table_steps_by_vector")
        a_tab = sem("table_steps_by_scalar")
        g_tab = sem("table_steps_by_pool")
        t_tab = sem("table_steps_by_tensor")
        s_pack = sem("pack_rows_moved")

        ids_loaded = [sem(f"ids_loaded{j}") for j in range(2)]
        oha_ready = sem("onehot_a_ready")
        gathered = sem("gathered")
        acc_ready = sem("acc_ready")
        tap = sem("conv_tap")
        conv_done = sem("conv_done")
        u_ready = sem("u_ready")
        xp_done = sem("x_proj_done")
        bcs_ready = sem("bc_rows_copied")
        abs_done = sem("abs_done")
        relu_ready = sem("relu_ready")
        exp_done = sem("exp_done")
        soft_ready = sem("soft_ready")
        dt_ready = sem("dt_ready")
        dtu_ready = sem("dtu_ready")
        bc_stored = sem("bc_rows_stored")
        u_stored = sem("u_stored")
        dt_stored = sem("dt_stored")
        dtu_stored = sem("dtu_stored")
        widx_loaded = [sem(f"weight_index_loaded{j}") for j in range(2)]
        prod_ready = sem("weight_product_ready")
        prod_used = sem("weight_product_used")
        ffw_ready = sem("weight_tile_copied")

        tile_loaded = [sem(f"tile_loaded{i}") for i in range(2)]
        b_loaded = [sem(f"b_loaded{g}") for g in range(GQ)]
        c_loaded = [sem(f"c_loaded{g}") for g in range(GQ)]
        idsb_loaded = sem("ids_b_loaded")
        state_clear = sem("state_cleared")
        da_ready = sem("decay_ready")
        dbu_ready = sem("dbu_ready")
        scanned = sem("quad_scanned")
        hc_ready = sem("hc_ready")
        hc_used = sem("hc_used")
        saved = sem("state_saved")
        yts_ready = sem("y_time_major_copied")
        ysum_ready = sem("y_plus_skip_ready")
        yg_ready = sem("y_gated_ready")
        ohb_ready = sem("onehot_b_ready")
        filled = sem("bank_filled")
        h2_ready = sem("h2_ready")
        stats_part = sem("ln_stats_part")
        stats_ready = sem("ln_stats_ready")
        bn_part = sem("ln_bn_stats_ready")
        var_ready = sem("ln_variance_ready")
        rstd_ready = sem("ln_rstd_ready")
        xn2_ready = sem("xn_ready")
        xn2t_ready = sem("xn_transposed")
        th_ready = sem("tanh_ready")
        sg_ready = sem("silu_ready")
        mid_ready = sem("mid_ready")
        osb_ready = sem("out_tile_ready")
        out_stored = [sem(f"out_stored{tb}") for tb in range(TBB)]

        pg = [psum[:, 2 * i:2 * i + 2, :].rearrange("p a b -> p (a b)") for i in range(2)]
        p_bc, p_dt, p_w = psum[:, 4, :], [psum[:, 5, :], psum[:, 6, :]], psum[:, 7, :]
        hq = [psum[:, 2 * i:2 * i + 2, :].rearrange("p a b -> p (a b)").rearrange("p (i t) -> p i t", i=QN)
              for i in range(2)]
        p_yt = psum[:, 4, :].rearrange("p (e b d) -> p e b d", e=2, b=TBB)
        shared = [psum[:, 5 + b, :] for b in range(NF)]

        VT = ((0, P), (1, V1))

        block = ctx.enter_context(nc.Block())

        @block.sync
        def _(sp):
            sp.dma_start(tab[:, 0, :], table[0:P, :]).then_inc(s_tab, 16)
            sp.dma_start(tab[0:V1, 1, :], table[P:V, :]).then_inc(s_tab, 16)
            for dst, src in ((nw, norm_w), (cb, conv_b), (dtw, dt_w), (dtb, dt_b), (dpar[:], d_par),
                             (a_neg[:], a_log)):
                sp.dma_start(dst, src).then_inc(s_w, 16)
            sp.dma_start(cw, conv_w).then_inc(s_w, 16)
            sp.dma_start(xpw, xp_wT.rearrange("(e p) s -> p e s", p=P)).then_inc(s_w, 16)
            sp.dma_start(lut_sb, lut.broadcast_to([P, LUTN])).then_inc(s_w, 16)
            sp.dma_start(inw, in_wT.rearrange("(c p) e -> p c e", p=P)).then_inc(s_in, 16)
            sp.dma_start(outw[:], out_wT.rearrange("(e p) d -> p e d", p=P)).then_inc(s_outw, 16)
            sp.wait_ge(v_tab, 20)
            for j in range(3):
                sp.dma_start(pack[V1 * j:V1 * (j + 1), :], lo_st[0:V1, j, 0:CX]).then_inc(s_pack, 16)
                sp.dma_start(xpack[V1 * j:V1 * (j + 1), :], lo_st[0:V1, j, CX:CT]).then_inc(s_pack, 16)

            sp.wait_ge(s_pack, 96)
            sp.dma_start(widx_sb[0], widx[0]).then_inc(widx_loaded[0], 16)
            with sp.Fori(0, NA // 2) as i:
                for j in range(2):
                    sp.wait_ge(oha_ready, 4 * i + 2 * j + 1)
                    sp.dma_start(idsa[j], ids_a[bass.ds(2 * i + j, 1), :].broadcast_to([P, TA + HALO])
                                 ).then_inc(ids_loaded[j], 16)
                for j in range(2):
                    for r in range(4):
                        t = 4 * j + r
                        sp.wait_ge(prod_ready, LUTN * 8 * i + LUTN * (t + 1))
                        sp.dma_start(widx_sb[(t + 1) % 2], widx[bass.ds(8 * i + (t + 1), 1), :, :].rearrange(
                            "a p c -> (a p) c")).then_inc(widx_loaded[(t + 1) % 2], 16)
                    if j == 0:
                        for jj in range(2):
                            sp.wait_ge(bcs_ready, 2 * i + (jj + 3))
                            sp.dma_start(bc[:, bass.ds(2 * TA * i + TA * jj, TA)], bcs[jj][0:2 * NS, :]
                                         ).then_inc(bc_stored, 16)
                            sp.wait_ge(u_ready, 16 * i + (8 * jj + 10))
                            sp.dma_start(chan[:, :, 2, bass.ds(2 * TA * i + TA * jj, TA)],
                                         u_sb[jj]).then_inc(u_stored, 16)
                    sp.wait_ge(dt_ready, 4 * i + 2 * (j + 1))
                    sp.dma_start(chan[:, :, 0, bass.ds(2 * TA * i + TA * j, TA)],
                                 relu).then_inc(dt_stored, 16)
                    sp.wait_ge(dtu_ready, 4 * i + (2 * j + 6))
                    sp.dma_start(chan[:, :, 1, bass.ds(2 * TA * i + TA * j, TA)],
                                 soft).then_inc(dtu_stored, 16)

            for s in (bc_stored, u_stored, dt_stored, dtu_stored):
                sp.wait_ge(s, 16 * (NA + 2))
            sp.wait_ge(prod_ready, LUTN * (WTILES + 1))
            sp.wait_ge(ffw_ready, WTILES + 1)
            with sp.Fori(0, NB) as k:
                for p in range(PAIRS):
                    sp.wait_ge(yg_ready, PAIRS * k + (PAIRS + p - 1))
                    sp.dma_start(tiles[p % 2].rearrange("p e a t -> p (e a) t"),
                                 chan[:, 2 * p:2 * p + 2, :, bass.ds(TB * k, TB)].rearrange("p e a t -> p (e a) t")
                                 ).then_inc(tile_loaded[p % 2], 16)
                    if p == 0:
                        for g in range(GQ):
                            last = QUADS - GQ + g + 1
                            sp.wait_ge(dbu_ready, QUADS * k + last)
                            sp.dma_start(b_rep[:, QN * g:QN * g + QN, :],
                                         bc[QN * g:QN * g + QN, bass.ds(TB * k, TB)].rearrange(
                                             "(a n) t -> a n t", a=1).broadcast_to([P, QN, TB])
                                         ).then_inc(b_loaded[g], 16)
                            sp.wait_ge(hc_ready, QUADS * k + last)
                            sp.dma_start(c_rep[:, QN * g:QN * g + QN, :],
                                         bc[NS + QN * g:NS + QN * g + QN, bass.ds(TB * k, TB)].rearrange(
                                             "(a n) t -> a n t", a=1).broadcast_to([P, QN, TB])
                                         ).then_inc(c_loaded[g], 16)
                        sp.wait_ge(ohb_ready, 2 * k + 2)
                        sp.dma_start(idsb, ids_b[bass.ds(k, 1), :].broadcast_to([P, TB])).then_inc(idsb_loaded, 16)
            for tb in range(TBB):
                sp.wait_ge(out_stored[tb], 16 * (NB + 2))

        @block.gpsimd
        def _(pool):
            nc.gpsimd.memset(ident[:], 0.0).then_inc(s_const, 1)
            nc.gpsimd.memset(eps_e[:], -0.5).then_inc(s_const, 1)
            nc.gpsimd.iota(row_i[:, 0:1], pattern=[[0, 1]], base=0, channel_multiplier=1).then_inc(s_const, 1)
            pool.wait_ge(s_const, 3)
            nc.gpsimd.affine_select(out=ident[:], in_=ident[:], compare_op=ALU.not_equal, fill=1.0, base=0,
                                    pattern=[[-1, P]], channel_multiplier=1).then_inc(s_const, 1)
            for c in range(2):
                for n, (t, r) in enumerate(VT):
                    pool.wait_ge(v_tab, (10, 16)[c])
                    src = stt[0:r, t, (8, 11)[c]:(9, 12)[c]]
                    nc.gpsimd.tensor_scalar(stt[0:r, t, 12:13], src, (1.0, 1.0 / DM)[c], EPS, ALU.mult,
                                            ALU.add).then_inc(g_tab, 1)
                    pool.wait_ge(g_tab, 4 * c + 2 * n + 1)
                    nc.gpsimd.tensor_tensor(stt[0:r, t, (9, 13)[c]:(10, 14)[c]], stt[0:r, t, 12:13], eps_e[0:r, :],
                                            ALU.pow).then_inc(g_tab, 1)

            pool.sem_inc(dbu_ready, QUADS)
            pool.sem_inc(rstd_ready, TBB)

            def rstd(k, tb):
                pool.wait_ge(stats_ready, TBB * k + (TBB + tb + 1))
                nc.gpsimd.tensor_tensor(st2[:, tb, 9:10], st2[:, tb, 8:9], eps_e[:, :], ALU.pow
                                        ).then_inc(rstd_ready, 1)

            def chunk(k, scan):
                for q in range(QUADS):
                    e, g = q // GQ, q % GQ
                    if scan:
                        par = (e // 2) % 2
                        if q % QP == 0:
                            pool.wait_ge(tile_loaded[par], 32 * k + 16 * (e // 4 + 1))
                        if e == 0:
                            pool.wait_ge(b_loaded[g], 16 * k + 16)
                        pool.wait_ge(scanned, QUADS * k + (QUADS + q - 1))
                        nc.gpsimd.tensor_tensor(
                            dbu[q % 2], tiles[par][:, e % 2, 1, :].rearrange("p (a t) -> p a t", a=1).broadcast_to(
                                [P, QN, TB]), b_rep[:, QN * g:QN * g + QN, :], ALU.mult).then_inc(dbu_ready, 1)
                    for t in POOL_PLAN[q]:
                        rstd(k, t[1])

            with pool.Fori(0, NB) as k:
                chunk(k, True)
            chunk(NB, False)

        @block.tensor
        def _(pe):
            pe.wait_ge(s_const, 4)
            pe.wait_ge(v_tab, 18)
            for t, r in VT:
                for c in range(DK):
                    mm = nc.tensor.transpose(psum[:, 5 + t, r * c:r * c + r], tmp[0:r, t, P * c:P * c + P],
                                             ident[0:r, 0:r])
                mm.then_inc(t_tab, 1)
            pe.wait_ge(a_tab, 2 + 2 * DK)
            pe.wait_ge(s_in, 16)
            for t, r in VT:
                for e in range(4):
                    n = 4 * t + e
                    if n >= 4:
                        pe.wait_ge(a_tab, 2 + 2 * DK + n - 3)
                    for c in range(DK):
                        mm = nc.tensor.matmul(psum[0:r, e, :], xnt[:, c, P * t:P * t + r],
                                              inw[:, c, 512 * e:512 * e + 512], start=(c == 0), stop=(c == DK - 1))
                    mm.then_inc(t_tab, 1)

            def weight_tile(i, t):
                pe.wait_ge(ffw_ready, 8 * i + (t + 1))
                for v in range(LUTN):
                    pe.wait_ge(prod_ready, LUTN * 8 * i + (LUTN * (t + 1) + v + 1))
                    for c in range(DK):
                        mm = nc.tensor.matmul(p_w[:, P * c:P * c + P], prod[v % 4][:, P * c:P * c + P], ident[:],
                                              is_transpose=True, start=(v == 0 and c == 0),
                                              stop=(v == LUTN - 1), skip_group_check=True)
                    mm.then_inc(prod_used, 1)

            def x_proj(i, j, e):
                pe.wait_ge(u_ready, 16 * i + (8 * j + e + 3))
                if e == 0:
                    pe.wait_ge(bcs_ready, 2 * i + (j + 2))
                    if j == 0:
                        pe.wait_ge(relu_ready, 16 * i + 16)
                nc.tensor.matmul(p_bc[0:2 * NS, :], xpw[:, e, 0:2 * NS], u_sb[j][:, e, :], start=(e == 0),
                                 stop=(e == ET - 1))
                nc.tensor.matmul(p_dt[j], xdtw[:, e, :], u_sb[j][:, e, :], start=(e == 0), stop=(e == ET - 1)
                                 ).then_inc(xp_done, 1)

            pe.wait_ge(a_tab, 2 + 2 * DK + 8 + 1)
            pe.wait_ge(v_tab, 20)
            pe.wait_ge(s_pack, 96)
            pe.sem_inc(prod_used, 4)
            with pe.Fori(0, NA // 2) as i:
                for j in range(2):
                    for e in range(ET):
                        if e == 0:
                            pe.wait_ge(oha_ready, 4 * i + (4 + 2 * (j + 1)))
                        pe.wait_ge(conv_done, 16 * i + (8 * j + e + 1))
                        cols = slice(P * e, P * e + P)
                        w = [xpart[:, m, cols] for m in range(3)] + [xpack[0:3 * V1, cols]]
                        for m in range(4):
                            oh = oha[j][:, 0, :] if m < 3 else oha[j][0:3 * V1, 1, :]
                            nc.tensor.matmul(pg[e % 2][:, 0:TA], w[m], oh[:, 0:TA], start=(m == 0), stop=(m == 3))
                        for m in range(4):
                            oh = oha[j][:, 0, :] if m < 3 else oha[j][0:3 * V1, 1, :]
                            mm = nc.tensor.matmul(pg[e % 2][:, TA:TA + HALO], w[m], oh[:, TA:TA + HALO],
                                                  start=(m == 0), stop=(m == 3))
                        mm.then_inc(gathered, 1)
                        n = 8 * j + e - 2
                        if n >= 0:
                            x_proj(i, n // 8, n % 8)
                for n in (14, 15):
                    x_proj(i, n // 8, n % 8)
                for t in range(8):
                    weight_tile(i, t)
            weight_tile(NA // 2, 0)

            pe.sem_inc(hc_used, QUADS)
            pe.sem_inc(filled, len(USES))

            def step(k, bk, t):
                name = t[0]
                use = t[:2]
                b = bk.bank(use)
                bank = shared[b]
                if len(t) < 3 or t[2] == 0:
                    (who, n), back = bk.previous(use)
                    done, per, at = {"op": (h2_ready, TBB, n + 1), "xt": (xn2t_ready, TBB, n + 1),
                                     "gu": (mid_ready, OT, n + 1), "dn": (osb_ready, TBB, n + 1),
                                     "yb": (ysum_ready, 2 * PAIRS, 2 * n + 2), "sz": (yg_ready, PAIRS, n + 1)}[who]
                    pe.wait_ge(done, per * k + (at if back else per + at))
                if name == "op":
                    tb, half = t[1], t[2]
                    tt = slice(P * tb, P * tb + P)
                    if half == 0:
                        if tb == 0:
                            pe.wait_ge(yg_ready, PAIRS * k + PAIRS)
                        for m in range(4):
                            oh = ohb[:, 0, tt] if m < 3 else ohb[0:3 * V1, 1, tt]
                            w = part[:, m, CB:CB + DM] if m < 3 else pack[0:3 * V1, CB:CB + DM]
                            nc.tensor.matmul(bank, oh, w, start=(m == 0), stop=False)
                    for e in range(ET // 2 * half, ET // 2 * (half + 1)):
                        mm = nc.tensor.matmul(bank, yg[:, e, tt], outw[:, e, :], start=False, stop=(e == ET - 1))
                    if half == 1:
                        mm.then_inc(filled, 1)
                elif name == "xt":
                    tb = t[1]
                    pe.wait_ge(xn2_ready, TBB * k + (TBB + tb + 1))
                    for c in range(DK):
                        mm = nc.tensor.matmul(bank[:, P * c:P * c + P], xn2[:, tb, P * c:P * c + P], ident[:],
                                              is_transpose=True, start=(c == 0), stop=(c == DK - 1),
                                              skip_group_check=True)
                    mm.then_inc(filled, 1)
                elif name == "gu":
                    o = t[1]
                    if o == 0:
                        pe.wait_ge(xn2t_ready, TBB * k + 2 * TBB)
                    for m in range(2):
                        for c in range(DK):
                            mm = nc.tensor.matmul(bank[:, TB * m:TB * m + TB], ffw[:, OT * m + o, P * c:P * c + P],
                                                  xn2t[:, c, :], start=(c == 0), stop=(c == DK - 1))
                    mm.then_inc(filled, 1)
                elif name == "dn":
                    tb, j = t[1], t[2]
                    for o in range(4 * j, min(4 * j + 4, OT)):
                        if tb == 0:
                            pe.wait_ge(mid_ready, OT * k + (OT + o + 1))
                        mm = nc.tensor.matmul(bank, mid[:, o, P * tb:P * tb + P], ffw[:, 2 * OT + o, :],
                                              start=(o == 0), stop=(o == OT - 1))
                    if j == 2:
                        mm.then_inc(filled, 1)
                elif name == "sz":
                    if t[1] == 0:
                        pe.wait_ge(ohb_ready, 2 * k + 4)
                    for e in range(2):
                        cols = slice(CZ + P * (2 * t[1] + e), CZ + P * (2 * t[1] + e + 1))
                        for m in range(4):
                            w = part[:, m, cols] if m < 3 else pack[0:3 * V1, cols]
                            oh = ohb[:, 0, :] if m < 3 else ohb[0:3 * V1, 1, :]
                            mm = nc.tensor.matmul(bank[:, TB * e:TB * e + TB], w, oh, start=(m == 0), stop=(m == 3))
                    mm.then_inc(filled, 1)
                elif name == "yb":
                    pe.wait_ge(yts_ready, PAIRS * k + (PAIRS + t[1] + 1))
                    for e in range(2):
                        for b2 in range(TBB):
                            mm = nc.tensor.matmul(bank[:, TB * e + P * b2:TB * e + P * b2 + P],
                                                  yts[:, e, P * b2:P * b2 + P], ident[:], is_transpose=True,
                                                  start=(e == 0 and b2 == 0), stop=(e == 1 and b2 == TBB - 1),
                                                  skip_group_check=True)
                    mm.then_inc(filled, 1)

            def chunk(k, scan):
                bk = Banks(scan)
                for q in range(QUADS + 1):
                    if scan and q < QUADS:
                        e = q // GQ
                        if q % QP == 0:
                            pe.wait_ge(yts_ready, PAIRS * k + (PAIRS + q // QP))
                        pe.wait_ge(hc_ready, QUADS * k + (QUADS + q + 1))
                        for i in range(QN):
                            for b2 in range(TBB):
                                mm = nc.tensor.matmul(p_yt[:, e % 2, b2, :], hc[q % NG][:, i, P * b2:P * b2 + P],
                                                      ident[:], is_transpose=True,
                                                      start=(q % QP == 0 and i == 0 and b2 == 0),
                                                      stop=(q % QP == QP - 1 and i == QN - 1 and b2 == TBB - 1),
                                                      skip_group_check=True)
                        mm.then_inc(hc_used, 1)
                    for t in PE_PLAN[q]:
                        if scan or t[0] not in SCAN_ONLY:
                            step(k, bk, t)

            pe.wait_ge(s_outw, 16)
            pe.wait_ge(ffw_ready, WTILES + 1)
            with pe.Fori(0, NB) as k:
                chunk(k, True)
            chunk(NB, False)

        @block.scalar
        def _(act):
            for n, (t, r) in enumerate(VT):
                act.wait_ge(v_tab, 4)
                nc.scalar.activation(tmp[0:r, t, :], tab[0:r, t, :], ACT.Exp, bias=stt[0:r, t, 1:2],
                                     accum_out=stt[0:r, t, 2:3]).then_inc(a_tab, 1)
            act.wait_ge(s_w, 16 * 9)
            for t, r in VT:
                act.wait_ge(t_tab, t + 1)
                for c in range(DK):
                    nc.scalar.activation(xnt[:, c, P * t:P * t + r], psum[:, 5 + t, r * c:r * c + r], ACT.Copy,
                                         scale=nw[:, c:c + 1]).then_inc(a_tab, 1)
            for t, r in VT:
                for e in range(4):
                    act.wait_ge(t_tab, 2 + 4 * t + e + 1)
                    if e < 2:
                        nc.scalar.activation(full[0:r, t, CX + 512 * e:CX + 512 * e + 512], psum[0:r, e, :],
                                             ACT.Copy).then_inc(a_tab, 1)
                    else:
                        nc.scalar.activation(full[0:r, t, CZ + 512 * (e - 2):CZ + 512 * (e - 1)], psum[0:r, e, :],
                                             ACT.Silu).then_inc(a_tab, 1)
            nc.scalar.activation(xdtw, xpw[:, :, 2 * NS:2 * NS + 1].broadcast_to([P, ET, P]), ACT.Copy
                                 ).then_inc(a_tab, 1)
            act.wait_ge(s_w, 16 * 9)
            nc.scalar.activation(a_neg[:], a_neg[:], ACT.Exp).then_inc(a_tab, 1)
            act.wait_ge(a_tab, 2 + 2 * DK + 8 + 2)
            nc.scalar.activation(a_neg[:], a_neg[:], ACT.Copy, scale=-1.0).then_inc(a_tab, 1)

            act.sem_inc(bcs_ready, 2)
            act.sem_inc(relu_ready, 16)
            act.sem_inc(u_ready, 2)
            act.sem_inc(ffw_ready, 1)

            def silu(i, j, e):
                act.wait_ge(conv_done, 16 * i + (8 * j + e + 3))
                if e == 0:
                    if j == 0:
                        act.wait_ge(dtu_ready, 4 * i + 4)
                        act.wait_ge(u_stored, 32 * i + 32)
                nc.scalar.activation(u_sb[j][:, e, :], pre[e % 2], ACT.Silu).then_inc(u_ready, 1)

            def copy_weight_tile(i, t):
                act.wait_ge(prod_used, LUTN * 8 * i + (LUTN * (t + 1) + 4))
                nc.scalar.activation(ffw[:, bass.ds(8 * i + t, 1), :].rearrange("p a c -> p (a c)")
                                     if not isinstance(i, int) else ffw[:, 8 * i + t, :], p_w, ACT.Copy
                                     ).then_inc(ffw_ready, 1)

            act.wait_ge(v_tab, 20)
            act.wait_ge(s_pack, 96)
            with act.Fori(0, NA // 2) as i:
                for n in range(17):
                    j, e = n // 8, n % 8
                    if n < 16:
                        act.wait_ge(gathered, 16 * i + n + 1)
                        act.wait_ge(conv_done, 16 * i + (n + 1))
                        nc.scalar.activation(acc[e % 2], pg[e % 2][:, HALO:HALO + TA], ACT.Identity,
                                             scale=cw[:, e, 3:4], bias=cb[:, e:e + 1]).then_inc(acc_ready, 1)
                    if n >= 1:
                        silu(i, (n - 1) // 8, (n - 1) % 8)
                    if n == 10:
                        act.wait_ge(xp_done, 16 * i + 8)
                        act.wait_ge(bc_stored, 32 * i + 32)
                        nc.scalar.activation(bcs[0][0:2 * NS, :], p_bc[0:2 * NS, :], ACT.Copy).then_inc(bcs_ready, 1)
                for j in range(2):
                    act.wait_ge(xp_done, 16 * i + 8 * (j + 1))
                    if j == 1:
                        nc.scalar.activation(bcs[1][0:2 * NS, :], p_bc[0:2 * NS, :], ACT.Copy).then_inc(bcs_ready, 1)
                    act.wait_ge(dt_stored, 32 * i + (32 + 16 * j))
                    act.wait_ge(dtu_stored, 32 * i + (32 + 16 * j))
                    for e in range(ET):
                        nc.scalar.activation(soft[:, e, :], p_dt[j], ACT.Abs, scale=dtw[:, e:e + 1],
                                             bias=dtb[:, e:e + 1]).then_inc(abs_done, 1)
                        nc.scalar.activation(relu[:, e, :], p_dt[j], ACT.Relu, scale=dtw[:, e:e + 1],
                                             bias=dtb[:, e:e + 1]).then_inc(relu_ready, 1)
                    for h in range(2):
                        s4 = soft[:, 4 * h:4 * h + 4, :]
                        act.wait_ge(abs_done, 16 * i + (8 * j + 4 * h + 4))
                        nc.scalar.activation(s4, s4, ACT.Exp, scale=-1.0).then_inc(exp_done, 1)
                    for h in range(2):
                        s4 = soft[:, 4 * h:4 * h + 4, :]
                        act.wait_ge(exp_done, 4 * i + (2 * j + h + 1))
                        nc.scalar.activation(s4, s4, ACT.Ln, bias=1.0).then_inc(soft_ready, 1)
                    for r in range(4):
                        copy_weight_tile(i, 4 * j + r)
            copy_weight_tile(NA // 2, 0)

            act.sem_inc(saved, 1)
            act.sem_inc(yts_ready, PAIRS)
            act.sem_inc(h2_ready, TBB)
            act.sem_inc(xn2t_ready, TBB)
            act.sem_inc(th_ready, OT)
            for tb in range(TBB):
                act.sem_inc(out_stored[tb], 16)

            def save(k, q):
                act.wait_ge(hc_ready, QUADS * k + (QUADS + q + 1))
                nc.scalar.activation(state[:, QN * q:QN * q + QN].rearrange("p (a b) -> p a b", b=1),
                                     hq[q % 2][:, :, TB - 1:TB], ACT.Copy).then_inc(saved, 1)

            def step(k, bk, t):
                name = t[0]
                if name == "h2":
                    tb = t[1]
                    b = bk.bank(("op", tb))
                    act.wait_ge(filled, len(USES) * k + (len(USES) + bk.filled(("op", tb))))
                    act.wait_ge(osb_ready, TBB * k + (tb + 1))
                    nc.scalar.activation(h2[:, tb, :], shared[b], ACT.Copy).then_inc(h2_ready, 1)
                elif name == "xnT":
                    tb = t[1]
                    b = bk.bank(("xt", tb))
                    act.wait_ge(filled, len(USES) * k + (len(USES) + bk.filled(("xt", tb))))
                    nc.scalar.activation(xn2t[:, :, P * tb:P * tb + P],
                                         shared[b].rearrange("p (c t) -> p c t", c=DK), ACT.Copy
                                         ).then_inc(xn2t_ready, 1)
                elif name == "tanh":
                    o = t[1]
                    b = bk.bank(("gu", o))
                    act.wait_ge(filled, len(USES) * k + (len(USES) + bk.filled(("gu", o))))
                    act.wait_ge(mid_ready, OT * k + (OT + o - 1))
                    nc.scalar.activation(th[o % 2], shared[b][:, 0:TB], ACT.Tanh, scale=0.5).then_inc(th_ready, 1)
                elif name == "yT":
                    p = t[1]
                    act.wait_ge(hc_used, QUADS * k + (QUADS + QP * (p + 1)))
                    if p > 0:
                        act.wait_ge(filled, len(USES) * k + (len(USES) + bk.filled(("yb", p - 1))))
                    nc.scalar.activation(yts, p_yt.rearrange("p e b d -> p (e b d)").rearrange(
                        "p (e t) -> p e t", e=2), ACT.Copy).then_inc(yts_ready, 1)
                elif name == "store":
                    tb = t[1]
                    act.wait_ge(osb_ready, TBB * k + (TBB + tb + 1))
                    if isinstance(k, int):
                        dst = out[P * (TBB * k + tb):P * (TBB * k + tb + 1), :]
                    else:
                        dst = out[bass.ds(TB * k + P * tb, P), :]
                    act.dma_start(dst, osb[:, tb, :]).then_inc(out_stored[tb], 16)

            def chunk(k, scan, store_k):
                bk = Banks(scan)
                for q in range(QUADS + 1):
                    if scan and q < QUADS:
                        e = q // GQ
                        par = (e // 2) % 2
                        if q % QP == 0:
                            act.wait_ge(tile_loaded[par], 32 * k + 16 * (e // 4 + 1))
                        if q >= 2:
                            save(k, q - 2)
                            act.wait_ge(saved, QUADS * k + q)
                        for i in range(QN):
                            n = NS * e + QN * (q % GQ) + i
                            nc.scalar.activation(hq[q % 2][:, i, :], tiles[par][:, e % 2, 0, :], ACT.Exp,
                                                 scale=a_neg[:, n:n + 1]).then_inc(da_ready, 1)
                    if scan and q == QUADS:
                        save(k, QUADS - 2)
                        save(k, QUADS - 1)
                        act.wait_ge(saved, QUADS * k + (QUADS + 1))
                    for t in ACT_PLAN[q]:
                        if scan or t[0] not in SCAN_ONLY:
                            if t[0] == "store" and not store_k:
                                continue
                            step(k, bk, t)

            act.wait_ge(conv_done, NA * ET + 2)
            with act.Fori(0, NB) as k:
                chunk(k, True, True)
            chunk(NB, False, True)

        @block.vector
        def _(dve):
            dve.wait_ge(s_const, 4)
            nc.vector.tensor_copy(rows[:, 0:1], row_i[:, 0:1]).then_inc(v_tab, 1)
            dve.wait_ge(v_tab, 1)
            dve.wait_ge(s_tab, 32)
            nc.vector.tensor_scalar(rows[:, 1:2], rows[:, 0:1], float(V1), -float(V1), ALU.is_ge, ALU.mult
                                    ).then_inc(v_tab, 1)
            for t, r in VT:
                nc.vector.reduce_max(stt[0:r, t, 0:1], tab[0:r, t, :], AX_X)
                nc.vector.engine_nop() if False else None
            nc.vector.tensor_scalar(stt[:, 0, 15:16], rows[:, 0:1], 2.0 * V1, -float(V1), ALU.is_ge, ALU.mult
                                    ).then_inc(stats_part, 1)
            dve.wait_ge(stats_part, 1)
            dve.wait_ge(v_tab, 2)
            for n, (t, r) in enumerate(VT):
                nc.vector.tensor_scalar(stt[0:r, t, 1:2], stt[0:r, t, 0:1], -1.0, None, ALU.mult).then_inc(v_tab, 1)
            nc.vector.tensor_tensor(rows[:, 1:2], rows[:, 1:2], rows[:, 0:1], ALU.add).then_inc(stats_part, 1)
            dve.wait_ge(stats_part, 2)
            nc.vector.tensor_scalar(rows[:, 1:2], rows[:, 1:2], stt[:, 0, 15:16], float(P), ALU.add, ALU.add
                                    ).then_inc(stats_part, 1)
            for n, (t, r) in enumerate(VT):
                dve.wait_ge(a_tab, n + 1)
                nc.vector.reciprocal(stt[0:r, t, 3:4], stt[0:r, t, 2:3]).then_inc(v_tab, 1)
                dve.wait_ge(v_tab, 4 + 3 * n + 1)
                nc.vector.tensor_scalar(tab[0:r, t, :], tmp[0:r, t, :], stt[0:r, t, 3:4], None, ALU.mult
                                        ).then_inc(v_tab, 1)
                dve.wait_ge(v_tab, 4 + 3 * n + 2)
                nc.vector.bn_stats(rest[0:r, 8 * t:8 * t + 6], tab[0:r, t, :]).then_inc(stats_part, 1)
                dve.wait_ge(stats_part, 3 + n + 1)
                nc.vector.bn_aggr(stt[0:r, t, 7:9], rest[0:r, 8 * t:8 * t + 6]).then_inc(v_tab, 1)
            for n, (t, r) in enumerate(VT):
                dve.wait_ge(v_tab, 10)
                dve.wait_ge(g_tab, 2 * n + 2)
                nc.vector.tensor_scalar(tmp[0:r, t, :], tab[0:r, t, :], stt[0:r, t, 7:8], stt[0:r, t, 9:10],
                                        ALU.subtract, ALU.mult).then_inc(v_tab, 1)
                dve.wait_ge(v_tab, 10 + 3 * n + 1)
                nc.vector.tensor_tensor(full[0:r, t, CB:CB + DM], tab[0:r, t, :], tmp[0:r, t, :], ALU.add
                                        ).then_inc(v_tab, 1)
                dve.wait_ge(v_tab, 10 + 3 * n + 2)
                nc.vector.tensor_tensor_reduce(tab[0:r, t, :], tmp[0:r, t, :], tmp[0:r, t, :], 1.0, 0.0, ALU.mult,
                                               ALU.add, stt[0:r, t, 11:12]).then_inc(v_tab, 1)
            for n, (t, r) in enumerate(VT):
                dve.wait_ge(g_tab, 4 + 2 * n + 2)
                nc.vector.tensor_scalar(tmp[0:r, t, :], tmp[0:r, t, :], stt[0:r, t, 13:14], None, ALU.mult
                                        ).then_inc(v_tab, 1)
            dve.wait_ge(a_tab, 2 + 2 * DK + 8)
            chain = [5]

            def link(ins):
                chain[0] += 1
                ins.then_inc(stats_part, 1)
                dve.wait_ge(stats_part, chain[0])

            for t, r in VT:
                for lo, hi, dst in ((0, CX, part), (CX, CT, xpart)):
                    d3 = [(dst[:, m, :] if t == 0 else lo_st[0:r, m, lo:hi]) for m in range(3)]
                    src, rem = full[0:r, t, lo:hi], rest[0:r, lo:hi]
                    link(nc.vector.tensor_copy(d3[0], src))
                    link(nc.vector.tensor_tensor(rem, src, d3[0], ALU.subtract))
                    link(nc.vector.tensor_copy(d3[1], rem))
                    link(nc.vector.tensor_tensor(d3[2], rem, d3[1], ALU.subtract))
                nc.vector.tensor_copy(stt[0:r, t, 14:15], stt[0:r, t, 13:14]).then_inc(v_tab, 1)

            dve.wait_ge(s_pack, 96)
            dve.sem_inc(oha_ready, 4)
            dve.sem_inc(conv_done, 2)
            dve.sem_inc(dtu_ready, 4)
            dve.sem_inc(prod_ready, LUTN)
            for s in (bc_stored, u_stored, dt_stored, dtu_stored):
                dve.sem_inc(s, 32)

            def products(i, t):
                dve.wait_ge(widx_loaded[t % 2], 64 * i + 16 * (t // 2 + 1))
                for v in range(LUTN):
                    dve.wait_ge(prod_used, LUTN * 8 * i + (LUTN * t + v + 1))
                    nc.vector.tensor_scalar(prod[v % 4], widx_sb[t % 2], float(v), lut_sb[:, v:v + 1], ALU.is_equal,
                                            ALU.mult).then_inc(prod_ready, 1)

            with dve.Fori(0, NA // 2) as i:
                for j in range(2):
                    dve.wait_ge(ids_loaded[j], 16 * i + 16)
                    dve.wait_ge(xp_done, 16 * i + 1) if False else None
                    for m in range(2):
                        nc.vector.tensor_scalar(oha[j][:, m, 0:TA + HALO], idsa[j], rows[:, m:m + 1], None,
                                                ALU.is_equal).then_inc(oha_ready, 1)
                for n in range(16):
                    e = n % 8
                    dve.wait_ge(acc_ready, 16 * i + n + 1)
                    dve.wait_ge(u_ready, 16 * i + (n + 1))
                    for m in (2, 1, 0):
                        src = acc[e % 2]
                        ins = nc.vector.scalar_tensor_tensor(
                            out=(pre[e % 2] if m == 0 else src), in0=pg[e % 2][:, m:m + TA], scalar=cw[:, e, m:m + 1],
                            in1=src, op0=ALU.mult, op1=ALU.add)
                        if m:
                            ins.then_inc(tap, 1)
                            dve.wait_ge(tap, 32 * i + (2 * n + 3 - m))
                        else:
                            ins.then_inc(conv_done, 1)
                for j in range(2):
                    for r in range(4):
                        products(i, 4 * j + r)
                    for h in range(2):
                        dve.wait_ge(soft_ready, 4 * i + (2 * j + h + 1))
                        s4, r4 = soft[:, 4 * h:4 * h + 4, :], relu[:, 4 * h:4 * h + 4, :]
                        nc.vector.tensor_tensor(r4, r4, s4, ALU.add).then_inc(dt_ready, 1)
                        dve.wait_ge(dt_ready, 4 * i + (2 * j + h + 1))
                        nc.vector.tensor_tensor(s4, r4, u_sb[j][:, 4 * h:4 * h + 4, :], ALU.mult
                                                ).then_inc(dtu_ready, 1)
            products(NA // 2, 0)

            dve.wait_ge(s_pack, 96)
            for s in (bc_stored, u_stored, dt_stored, dtu_stored):
                dve.wait_ge(s, 16 * (NA + 2))
            dve.wait_ge(ffw_ready, WTILES + 1)
            for z in (yg, ohb.bitcast(F32) if False else ohb, idsb):
                nc.vector.memset(z, 0.0 if z is not idsb else 0).then_inc(tap, 1)
            dve.wait_ge(tap, 32 * (NA // 2) + 3)
            dve.sem_inc(scanned, QUADS)
            dve.sem_inc(hc_ready, QUADS)
            dve.sem_inc(yg_ready, PAIRS)
            dve.sem_inc(ysum_ready, 2 * PAIRS)
            dve.sem_inc(ohb_ready, 2)
            dve.sem_inc(bn_part, TBB)
            dve.sem_inc(var_ready, TBB)
            dve.sem_inc(stats_ready, TBB)
            dve.sem_inc(xn2_ready, TBB)
            dve.sem_inc(sg_ready, OT)
            dve.sem_inc(mid_ready, OT)
            dve.sem_inc(osb_ready, TBB)

            def step(k, bk, t):
                name = t[0]
                if name == "stats":
                    tb = t[1]
                    dve.wait_ge(h2_ready, TBB * k + (TBB + tb + 1))
                    nc.vector.bn_stats(st2[:, tb, 0:6], h2[:, tb, :]).then_inc(bn_part, 1)
                    dve.wait_ge(s_const, 4)
                    dve.wait_ge(bn_part, TBB * k + (TBB + tb + 1))
                    nc.vector.bn_aggr(st2[:, tb, 6:8], st2[:, tb, 0:6]).then_inc(var_ready, 1)
                    dve.wait_ge(var_ready, TBB * k + (TBB + tb + 1))
                    nc.vector.tensor_scalar(st2[:, tb, 8:9], st2[:, tb, 7:8], EPS, None, ALU.add
                                            ).then_inc(stats_ready, 1)
                elif name == "norm":
                    tb = t[1]
                    dve.wait_ge(rstd_ready, TBB * k + (TBB + tb + 1))
                    nc.vector.tensor_scalar(xn2[:, tb, :], h2[:, tb, :], st2[:, tb, 6:7], st2[:, tb, 9:10],
                                            ALU.subtract, ALU.mult).then_inc(xn2_ready, 1)
                elif name == "onehot":
                    dve.wait_ge(idsb_loaded, 16 * k + 16)
                    dve.wait_ge(filled, len(USES) * k + (len(USES) + bk.filled(("op", TBB - 1))))
                    for m in range(2):
                        nc.vector.tensor_scalar(ohb[:, m, :], idsb, rows[:, m:m + 1], None, ALU.is_equal
                                                ).then_inc(ohb_ready, 1)
                elif name == "mid":
                    o = t[1]
                    b = bk.bank(("gu", o))
                    dve.wait_ge(th_ready, OT * k + (OT + o + 1))
                    dve.wait_ge(mid_ready, OT * k + (OT + o))
                    nc.vector.scalar_tensor_tensor(out=sg, in0=th[o % 2], scalar=1.0, in1=shared[b][:, 0:TB],
                                                   op0=ALU.add, op1=ALU.mult).then_inc(sg_ready, 1)
                    dve.wait_ge(sg_ready, OT * k + (OT + o + 1))
                    nc.vector.scalar_tensor_tensor(out=mid[:, o, :], in0=sg, scalar=0.5, in1=shared[b][:, TB:2 * TB],
                                                   op0=ALU.mult, op1=ALU.mult).then_inc(mid_ready, 1)
                elif name == "out":
                    tb = t[1]
                    b = bk.bank(("dn", tb))
                    dve.wait_ge(filled, len(USES) * k + (len(USES) + bk.filled(("dn", tb))))
                    dve.wait_ge(out_stored[tb], 16 * k + 16)
                    nc.vector.tensor_tensor(osb[:, tb, :], h2[:, tb, :], shared[b], ALU.add).then_inc(osb_ready, 1)
                elif name == "fin":
                    p = t[1]
                    b, bz = bk.bank(("yb", p)), bk.bank(("sz", p))
                    dve.wait_ge(filled, len(USES) * k + (len(USES) + bk.filled(("yb", p))))
                    for e in range(2):
                        nc.vector.scalar_tensor_tensor(
                            out=ysum[:, e, :], in0=tiles[p % 2][:, e, 2, :], scalar=dpar[:, 2 * p + e:2 * p + e + 1],
                            in1=shared[b][:, TB * e:TB * e + TB], op0=ALU.mult, op1=ALU.add).then_inc(ysum_ready, 1)
                    dve.wait_ge(ysum_ready, 2 * PAIRS * k + (2 * PAIRS + 2 * p + 2))
                    nc.vector.tensor_tensor(yg[:, 2 * p:2 * p + 2, :], ysum,
                                            shared[bz].rearrange("p (e t) -> p e t", e=2), ALU.mult
                                            ).then_inc(yg_ready, 1)

            def chunk(k, scan):
                bk = Banks(scan)
                if scan:
                    dve.wait_ge(saved, QUADS * k + 1)
                for q in range(QUADS + 1):
                    if scan and q < QUADS:
                        e, g = q // GQ, q % GQ
                        dve.wait_ge(dbu_ready, QUADS * k + (QUADS + q + 1))
                        for i in range(QN):
                            n = NS * e + QN * g + i
                            if i % 2 == 0:
                                dve.wait_ge(da_ready, NS * ET * k + (QN * q + i + 2))
                            h = hq[q % 2][:, i, :]
                            ins = nc.vector.tensor_tensor_scan(h, h, dbu[q % 2][:, i, :], state[:, n:n + 1],
                                                               ALU.mult, ALU.add)
                        ins.then_inc(scanned, 1)
                        if e == 0:
                            dve.wait_ge(c_loaded[g], 16 * k + 16)
                        dve.wait_ge(hc_used, QUADS * k + (QUADS + q + 1 - NG))
                        dve.wait_ge(scanned, QUADS * k + (QUADS + q + 1))
                        nc.vector.tensor_tensor(hc[q % NG], hq[q % 2], c_rep[:, QN * g:QN * g + QN, :], ALU.mult
                                                ).then_inc(hc_ready, 1)
                    for t in DVE_PLAN[q]:
                        if scan or t[0] not in SCAN_ONLY:
                            step(k, bk, t)

            with dve.Fori(0, NB // CPB) as s:
                dve.wait_ge(saved, NB // 2 * QUADS * s + 1)
                nc.vector.memset(state[:], 0.0).then_inc(state_clear, 1)
                with dve.Fori(0, CPB) as c:
                    dve.wait_ge(state_clear, s + 1)
                    chunk(s * CPB + c, True)
            chunk(NB, False)


def kernel(x, L0_tok_catid_time_matrix, L0_attn_norm_w, L0_attn_in_proj_w, L0_attn_conv_w, L0_attn_conv_b,
           L0_attn_x_proj_w, L0_attn_dt_w, L0_attn_dt_b, L0_attn_A_log, L0_attn_D_param, L0_attn_out_proj_w,
           L0_ffn_lut, L0_ffn_gate_idx, L0_ffn_up_idx, L0_ffn_down_idx):
    import numpy as np
    import concourse.bacc as bacc
    from concourse.bass_utils import run_bass_kernel_spmd

    def cols(v):
        v = np.asarray(v)
        return np.ascontiguousarray(v.reshape(-1, P).T)

    x = np.asarray(x)
    padded = np.pad(x, ((0, 0), (HALO, 0)), constant_values=-1)
    ids_a = np.stack([padded[b, TA * c:TA * c + TA + HALO] for b in range(2) for c in range(SEQ // TA)])
    pad = OT * P - FF
    gate = np.pad(np.asarray(L0_ffn_gate_idx), ((0, pad), (0, 0)), constant_values=-1).reshape(OT, P, DM)
    up = np.pad(np.asarray(L0_ffn_up_idx), ((0, pad), (0, 0)), constant_values=-1).reshape(OT, P, DM)
    down = np.pad(np.asarray(L0_ffn_down_idx), ((0, 0), (0, pad)), constant_values=-1)
    down = down.reshape(DK, P, OT, P).transpose(2, 1, 0, 3).reshape(OT, P, DM)
    arrays = {
        "ids_a": ids_a,
        "ids_b": x.reshape(NB, TB),
        "table": np.asarray(L0_tok_catid_time_matrix),
        "norm_w": cols(L0_attn_norm_w),
        "in_wT": np.asarray(L0_attn_in_proj_w).T,
        "conv_w": np.asarray(L0_attn_conv_w).reshape(ET, P, 4).transpose(1, 0, 2),
        "conv_b": cols(L0_attn_conv_b),
        "xp_wT": np.asarray(L0_attn_x_proj_w).T,
        "dt_w": cols(np.asarray(L0_attn_dt_w).reshape(-1)),
        "dt_b": cols(L0_attn_dt_b),
        "a_log": np.asarray(L0_attn_A_log).reshape(ET, P, NS).transpose(1, 0, 2).reshape(P, ET * NS),
        "d_par": cols(L0_attn_D_param),
        "out_wT": np.asarray(L0_attn_out_proj_w).T,
        "lut": np.asarray(L0_ffn_lut).reshape(1, LUTN),
        "widx": np.concatenate([gate, up, down]),
    }
    arrays = {n: np.ascontiguousarray(a) for n, a in arrays.items()}
    nc = bacc.Bacc("TRN2", target_bir_lowering=False, num_devices=1)
    args = [nc.dram_tensor(n, a.shape, mybir.dt.from_np(a.dtype), kind="ExternalInput").ap()
            for n, a in arrays.items()]
    out = nc.dram_tensor("out", (TOK + TB, DM), F32, kind="ExternalOutput").ap()
    lm_tower_kernel(nc, *args, out)
    r = run_bass_kernel_spmd(nc, [arrays], core_ids=[0])
    return np.asarray(r.results[0]["out"])[TB:].reshape(2, SEQ, DM)
```

```python
from contextlib import ExitStack

import concourse.bass as bass
from concourse import mybir

F32 = mybir.dt.float32
BF16 = mybir.dt.bfloat16
I32 = mybir.dt.int32
ALU = mybir.AluOpType
ACT = mybir.ActivationFunctionType
AX_X = mybir.AxisListType.X

P = 128
V = 168
V1 = V - P
DM = 512
DK = DM // P
DI = 1024
ET = DI // P
NS = 16
TOK = 4096
SEQ = 2048
LUTN = 16
FF = 1376
OT = (FF + P - 1) // P
WTILES = 3 * OT
EPS = 1e-5

TA = 512
HALO = 3
NA = TOK // TA
WPC = (WTILES - 1) // NA
TB = 256
NB = TOK // TB
CPB = SEQ // TB
TBB = TB // P
QN = 4
GQ = NS // QN
QUADS = ET * GQ
PAIRS = ET // 2
QP = 2 * GQ
NG = 3
NF = 3
LAG = 2

CB, CZ, CX = 0, DM, DM + DI
CT = DM + 2 * DI


def quad(q):
    return 2 * (q // QP) + q % 2, (q % QP) // 2


def plan():
    pe, act, dve, pool = ({s: [] for s in range(QUADS)} for _ in range(4))
    for n, s in enumerate([1, 1, 2, 3, 3, 4, 5, 5]):
        pe[s] += [("op", n // 4, n % 4)]
    for tb, s in enumerate([5, 7]):
        act[s] += [("h2", tb)]
        dve[s + 1] += [("stats", tb)]
        pool[s + 3] += [("rstd", tb)]
        dve[s + 3] += [("norm", tb)]
        pe[s + 4] += [("xt", tb)]
        act[s + 6] += [("xnT", tb)]
    dve[7] += [("onehot",)]
    for n, s in enumerate([6, 7, 7, 8, 8, 9, 10, 10, 11, 12, 13, 13]):
        pe[s] += [("dn", n // 6, n % 6)]
    for tb in range(TBB):
        dve[11 + 4 * tb] += [("out", tb)]
        act[13 + 4 * tb] += [("store", tb)]
        act[22 + 3 * tb] += [("keep", tb)]
    for n, s in enumerate([14, 14, 15, 16, 16, 17, 17, 18, 20, 21, 21, 22, 22, 23, 24, 24, 25, 25, 26, 26, 28, 29]):
        pe[s] += [("gu", n // 2, n % 2)]
        if n % 2:
            act[s + 2] += [("tanh", n // 2)]
            pool[min(s + 3, QUADS - 1)] += [("mid", n // 2)]
    for p in range(-1, PAIRS - 1):
        s = QP * p + QP
        act[s + 1] += [("yT", p)]
        s += (0, 4, 3, 3)[p + 1]
        pe[s] += [("sz", p), ("yb", p)]
        dve[s + 1] += [("fin", p)]
    return pe, act, dve, pool


PE_PLAN, ACT_PLAN, DVE_PLAN, POOL_PLAN = plan()
PARTS = {"op": 4, "dn": 6, "gu": 2}


def wanted(t, scan, ffn):
    if t[0] in ("sz", "yb", "yT", "fin"):
        return scan or (ffn and t[1] < 0)
    if t[0] == "onehot":
        return scan
    if t[0] in ("dn", "out", "store"):
        return True
    return ffn


def bank_uses(scan, ffn):
    seq = []
    for s in range(QUADS):
        for t in PE_PLAN[s]:
            if wanted(t, scan, ffn) and t[:2] not in seq:
                seq.append(t[:2])
    return seq


def slot(plan, step):
    return [s for s in range(QUADS) if step in plan[s]][0]


def released(use):
    name, n = use
    step, plan = {"op": ("h2", ACT_PLAN), "xt": ("xnT", ACT_PLAN), "gu": ("tanh", ACT_PLAN), "dn": ("out", DVE_PLAN),
                  "yb": ("fin", DVE_PLAN), "sz": ("fin", DVE_PLAN)}[name]
    return slot(plan, (step, n))


class Banks:

    KINDS = {"loop": (True, True), "ffn": (False, True), "down": (False, False)}

    def __init__(self, turn):
        self.turn = turn
        self.seq, self.banks = self.assign(turn)
        self.before = self.assign({"loop": "loop", "ffn": "loop", "down": "ffn"}[turn])
        self.done = [t[:2] for s in range(QUADS) for t in PE_PLAN[s]
                     if t[:2] in self.seq and (t[0] not in PARTS or t[2] == PARTS[t[0]] - 1)]

    def assign(self, turn):
        seq, banks, free = bank_uses(*self.KINDS[turn]), [], [b - NF for b in range(NF)]
        for use in seq:
            b = free.index(min(free))
            banks.append(b)
            free[b] = released(use)
        return seq, banks

    def bank(self, use):
        return self.banks[self.seq.index(use)]

    def filled(self, k, use):
        n = self.done.index(use) + 1
        full = len(bank_uses(True, True))
        if self.turn == "down":
            return full * k + len(self.before[0]) + n
        return full * k + (full + n)

    def previous(self, use):
        n = self.seq.index(use)
        b = self.banks[n]
        for m in range(n - 1, -1, -1):
            if self.banks[m] == b:
                return self.seq[m], 0
        seq, banks = self.before
        return [u for u, c in zip(seq, banks) if c == b][-1], 1


def lm_tower_kernel(nc, ids_a, ids_b, table, norm_w, in_wT, conv_w, conv_b, xp_wT, dt_w, dt_b, a_log,
                    d_par, out_wT, lut, widx, out):
    chan = nc.dram_tensor("chan", [P, ET, 2, TOK], F32, kind="Internal").ap()
    bc = nc.dram_tensor("bc", [2 * NS, TOK], F32, kind="Internal").ap()

    with ExitStack() as ctx:
        def sb(name, shape, dt):
            return ctx.enter_context(nc.sbuf_tensor(name, shape, dt))

        def sem(name):
            return ctx.enter_context(nc.semaphore(name))

        ffw = sb("ffw", [P, WTILES, DM], F32)
        outw = sb("outw", [P, ET, DM], F32)
        part = sb("part", [P, 3, CX], BF16)
        pack = sb("pack", [P, CX], BF16)
        a_neg = sb("a_neg", [P, ET * NS], F32)
        dpar = sb("dpar", [P, ET], F32)
        ident = sb("ident", [P, P], F32)
        rows = sb("rows", [P, 2], F32)
        eps_e = sb("eps_e", [P, 1], F32)
        state = sb("state", [P, ET * NS], F32)
        work = sb("work", [P, 28640], F32)
        psum = ctx.enter_context(nc.psum_tensor("psum", [P, 8, 512], F32))

        class Region:

            def __init__(self, at=0):
                self.at = at

            def cut(self, shape, dt=F32):
                n = 1
                for d in shape:
                    n *= d
                words = (n * (2 if dt == BF16 else 4) + 3) // 4
                assert self.at + words <= 28640, self.at + words
                v = work[:, self.at:self.at + words]
                self.at += words
                if dt != F32:
                    v = v.bitcast(dt)
                    v = v[:, 0:n]
                if len(shape) == 2:
                    v = v.rearrange("p (a b) -> p a b", b=shape[1])
                elif len(shape) == 3:
                    v = v.rearrange("p (a b c) -> p a b c", b=shape[1], c=shape[2])
                return v

        ra = Region()
        u_sb = ra.cut([ET, TA])
        soft = ra.cut([ET, TA])
        relu = ra.cut([ET, TA])
        ra.at = 16384
        xpart = ra.cut([3, DI], BF16)
        xpack = ra.cut([DI], BF16)
        xpw = ra.cut([ET, 2 * NS + 1])
        pick = ra.cut([P])
        idsa = ra.cut([TA + HALO], I32)
        stage_a_buffers = ra.at
        oha = ra.cut([2, TA + HALO + 1], BF16)
        acc = [ra.cut([TA]) for _ in range(2)]
        pre = [ra.cut([TA]) for _ in range(2)]
        bcs = ra.cut([TA])
        widx_sb = [ra.cut([DM], I32) for _ in range(2)]
        prod = [ra.cut([DM]) for _ in range(4)]
        ra.at = max(ra.at, stage_a_buffers + 2 * DM + DK * V + 2 * DM + 3 * CT // 2 + 32)
        lut_sb = ra.cut([LUTN])
        cw = ra.cut([ET, 4])
        cb = ra.cut([ET])
        dtw = ra.cut([ET])
        dtb = ra.cut([ET])
        nw = ra.cut([DK])
        row_i = ra.cut([2], I32)
        rt = Region()
        inw = rt.cut([DK, 2 * DI])
        full = rt.cut([2, CT])
        rest = rt.cut([CT])
        rs2 = Region(stage_a_buffers)
        tab = rs2.cut([2, DM])
        xnt = rs2.cut([DK, V])
        tmp = rs2.cut([2, DM])
        lo_st = rs2.cut([3, CT], BF16)
        stt = rs2.cut([2, 16])

        rb = Region()
        b_rep = rb.cut([NS, TB])
        c_rep = rb.cut([NS, TB])
        tiles = [rb.cut([2, 2, TB]) for _ in range(2)]
        dtu = [rb.cut([2, TB]) for _ in range(2)]
        dbu = [rb.cut([QN, TB]) for _ in range(2)]
        hc = [rb.cut([QN, TB]) for _ in range(NG)]
        yts = rb.cut([2, TBB * P])
        ysum = rb.cut([2, TB])
        yg = rb.cut([ET, TB])
        h2 = rb.cut([TBB, DM])
        xn2 = rb.cut([TBB, DM])
        xn2t = rb.cut([DK, TB])
        mid = rb.cut([OT, TB])
        gus = [rb.cut([2, TB]) for _ in range(2)]
        th = rb.cut([TB])
        gxu = rb.cut([TB])
        osb = rb.cut([TBB, DM])
        ohb = rb.cut([2, TB], BF16)
        idsb = rb.cut([TB], I32)
        st2 = rb.cut([TBB, 16])

        s_const = sem("constants_built")
        s_w = sem("small_weights_loaded")
        s_in = sem("in_proj_loaded")
        s_outw = sem("out_proj_loaded")
        s_tab = sem("table_loaded")
        v_tab = sem("table_steps_by_vector")
        a_tab = sem("table_steps_by_scalar")
        g_tab = sem("table_steps_by_pool")
        t_tab = sem("table_steps_by_tensor")
        s_pack = sem("pack_rows_moved")

        ids_loaded = sem("ids_loaded")
        oha_ready = sem("onehot_a_ready")
        gathered = sem("gathered")
        acc_ready = sem("acc_ready")
        tap = sem("conv_tap")
        conv_done = sem("conv_done")
        u_ready = sem("u_ready")
        xp_done = sem("x_proj_done")
        abs_done = sem("abs_done")
        relu_ready = sem("relu_ready")
        dtrow_ready = sem("dt_row_copied")
        dtrow_done = sem("dt_row_spread")
        exp_done = sem("exp_done")
        soft_ready = sem("soft_ready")
        dt_ready = sem("dt_ready")
        bc_stored = sem("bc_rows_stored")
        u_stored = sem("u_stored")
        dt_stored = sem("dt_stored")
        widx_loaded = [sem(f"weight_index_loaded{j}") for j in range(2)]
        prod_ready = sem("weight_product_ready")
        prod_used = sem("weight_product_used")
        ffw_ready = sem("weight_tile_copied")

        b_start = sem("stage_b_start")
        tile_loaded = [sem(f"tile_loaded{i}") for i in range(2)]
        b_loaded = [sem(f"b_loaded{g}") for g in range(GQ)]
        c_loaded = [sem(f"c_loaded{g}") for g in range(GQ)]
        idsb_loaded = sem("ids_b_loaded")
        state_clear = sem("state_cleared")
        da_ready = sem("decay_ready")
        dbu_ready = sem("dbu_ready")
        dtu_ready = sem("dtu_ready")
        scanned = sem("quad_scanned")
        hc_ready = sem("hc_ready")
        hc_used = sem("hc_used")
        saved = sem("state_saved")
        yts_ready = sem("y_time_major_copied")
        ysum_ready = sem("y_plus_skip_ready")
        yg_ready = sem("y_gated_ready")
        ohb_ready = sem("onehot_b_ready")
        filled = sem("bank_filled")
        h2_ready = sem("h2_ready")
        stats_part = sem("ln_stats_part")
        stats_ready = sem("ln_stats_ready")
        bn_part = sem("ln_bn_stats_ready")
        var_ready = sem("ln_variance_ready")
        rstd_ready = sem("ln_rstd_ready")
        xn2_ready = sem("xn_ready")
        xn2t_ready = sem("xn_transposed")
        th_ready = sem("tanh_ready")
        gate_up_ready = sem("gate_up_copied")
        sigmoid_ready = sem("sigmoid_ready")
        gate_x_up = sem("gate_times_up_ready")
        mid_ready = sem("mid_ready")
        kept = sem("h2_kept")
        osb_ready = sem("out_tile_ready")
        out_stored = [sem(f"out_stored{tb}") for tb in range(TBB)]

        pg = [psum[:, 2 * i:2 * i + 2, :].rearrange("p a b -> p (a b)") for i in range(2)]
        p_bc, p_dt, p_w = psum[:, 4, :], psum[:, 5, :], [psum[:, 6, :], psum[:, 7, :]]
        hq = [psum[:, 2 * i:2 * i + 2, :].rearrange("p a b -> p (a b)").rearrange("p (i t) -> p i t", i=QN)
              for i in range(2)]
        p_yt = psum[:, 4, :].rearrange("p (e b d) -> p e b d", e=2, b=TBB)
        shared = [psum[:, 5 + b, :] for b in range(NF)]

        VT = ((0, P), (1, V1))

        block = ctx.enter_context(nc.Block())

        @block.sync
        def _(sp):
            sp.dma_start(tab[:, 0, :], table[0:P, :]).then_inc(s_tab, 16)
            sp.dma_start(tab[0:V1, 1, :], table[P:V, :]).then_inc(s_tab, 16)
            for dst, src in ((nw, norm_w), (cb, conv_b), (dtw, dt_w), (dtb, dt_b), (dpar[:], d_par),
                             (a_neg[:], a_log)):
                sp.dma_start(dst, src).then_inc(s_w, 16)
            sp.dma_start(cw, conv_w).then_inc(s_w, 16)
            sp.dma_start(xpw, xp_wT.rearrange("(e p) s -> p e s", p=P)).then_inc(s_w, 16)
            sp.dma_start(lut_sb, lut.broadcast_to([P, LUTN])).then_inc(s_w, 16)
            sp.dma_start(inw, in_wT.rearrange("(c p) e -> p c e", p=P)).then_inc(s_in, 16)
            sp.dma_start(outw[:], out_wT.rearrange("(e p) d -> p e d", p=P)).then_inc(s_outw, 16)
            sp.wait_ge(v_tab, 20)
            for j in range(3):
                sp.dma_start(pack[V1 * j:V1 * (j + 1), :], lo_st[0:V1, j, 0:CX]).then_inc(s_pack, 16)
                sp.dma_start(xpack[V1 * j:V1 * (j + 1), :], lo_st[0:V1, j, CX:CT]).then_inc(s_pack, 16)

            sp.wait_ge(s_pack, 96)
            sp.dma_start(widx_sb[0], widx[0]).then_inc(widx_loaded[0], 16)
            with sp.Fori(0, NA) as i:
                sp.wait_ge(oha_ready, 2 * i + 2)
                sp.dma_start(idsa, ids_a[bass.ds(i, 1), :].broadcast_to([P, TA + HALO])).then_inc(ids_loaded, 16)
                for t in range(WPC):
                    sp.wait_ge(prod_ready, LUTN * WPC * i + LUTN * (t + 1))
                    sp.dma_start(widx_sb[(t + 1) % 2], widx[bass.ds(WPC * i + (t + 1), 1), :, :].rearrange(
                        "a p c -> (a p) c")).then_inc(widx_loaded[(t + 1) % 2], 16)
                sp.wait_ge(dt_ready, 2 * i + 2)
                sp.dma_start(chan[:, :, 0, bass.ds(TA * i, TA)], relu).then_inc(dt_stored, 16)

            for s in (bc_stored, u_stored, dt_stored):
                sp.wait_ge(s, 16 * (NA + 1))
            sp.wait_ge(prod_ready, LUTN * (WTILES + 1))
            sp.wait_ge(ffw_ready, WTILES + 2)
            sp.wait_ge(b_start, 1)
            with sp.Fori(0, NB) as k:
                for p in range(PAIRS):
                    sp.wait_ge(yg_ready, PAIRS * k + (PAIRS + p - 1))
                    sp.dma_start(tiles[p % 2].rearrange("p e a t -> p (e a) t"),
                                 chan[:, 2 * p:2 * p + 2, :, bass.ds(TB * k, TB)].rearrange("p e a t -> p (e a) t")
                                 ).then_inc(tile_loaded[p % 2], 16)
                    if p == 0:
                        for g in range(GQ):
                            last = QUADS - QP + 2 * g + 2
                            sp.wait_ge(dbu_ready, QUADS * k + last)
                            sp.dma_start(b_rep[:, QN * g:QN * g + QN, :],
                                         bc[QN * g:QN * g + QN, bass.ds(TB * k, TB)].rearrange(
                                             "(a n) t -> a n t", a=1).broadcast_to([P, QN, TB])
                                         ).then_inc(b_loaded[g], 16)
                            sp.wait_ge(hc_ready, QUADS * k + last)
                            sp.dma_start(c_rep[:, QN * g:QN * g + QN, :],
                                         bc[NS + QN * g:NS + QN * g + QN, bass.ds(TB * k, TB)].rearrange(
                                             "(a n) t -> a n t", a=1).broadcast_to([P, QN, TB])
                                         ).then_inc(c_loaded[g], 16)
                        sp.wait_ge(ohb_ready, 2 * k + 2)
                        sp.dma_start(idsb, ids_b[bass.ds(k, 1), :].broadcast_to([P, TB])).then_inc(idsb_loaded, 16)
            for tb in range(TBB):
                sp.wait_ge(out_stored[tb], 16 * (NB + LAG + 1))

        @block.gpsimd
        def _(pool):
            nc.gpsimd.memset(ident[:], 0.0).then_inc(s_const, 1)
            nc.gpsimd.memset(eps_e[:], -0.5).then_inc(s_const, 1)
            nc.gpsimd.memset(pick[0:2 * NS, :], 0.0).then_inc(s_const, 1)
            nc.gpsimd.iota(row_i[:, 0:1], pattern=[[0, 1]], base=0, channel_multiplier=1).then_inc(s_const, 1)
            pool.wait_ge(s_const, 4)
            nc.gpsimd.memset(pick[2 * NS:2 * NS + 1, :], 1.0).then_inc(s_const, 1)
            pool.wait_ge(s_const, 5)
            nc.gpsimd.affine_select(out=ident[:], in_=ident[:], compare_op=ALU.not_equal, fill=1.0, base=0,
                                    pattern=[[-1, P]], channel_multiplier=1).then_inc(s_const, 1)
            for c in range(2):
                for n, (t, r) in enumerate(VT):
                    pool.wait_ge(v_tab, (10, 16)[c])
                    src = stt[0:r, t, (8, 11)[c]:(9, 12)[c]]
                    nc.gpsimd.tensor_scalar(stt[0:r, t, 12:13], src, (1.0, 1.0 / DM)[c], EPS, ALU.mult,
                                            ALU.add).then_inc(g_tab, 1)
                    pool.wait_ge(g_tab, 4 * c + 2 * n + 1)
                    nc.gpsimd.tensor_tensor(stt[0:r, t, (9, 13)[c]:(10, 14)[c]], stt[0:r, t, 12:13], eps_e[0:r, :],
                                            ALU.pow).then_inc(g_tab, 1)

            with pool.Fori(0, NA) as i:
                for h in range(2):
                    pool.wait_ge(soft_ready, 2 * i + (h + 1))
                    r4 = relu[:, 4 * h:4 * h + 4, :]
                    nc.gpsimd.tensor_tensor(r4, r4, soft[:, 4 * h:4 * h + 4, :], ALU.add).then_inc(dt_ready, 1)

            pool.wait_ge(b_start, 1)
            pool.sem_inc(dbu_ready, QUADS)
            pool.sem_inc(rstd_ready, TBB)
            pool.sem_inc(mid_ready, OT)

            def rstd(k, tb):
                pool.wait_ge(stats_ready, TBB * k + (TBB + tb + 1))
                nc.gpsimd.tensor_tensor(st2[:, tb, 9:10], st2[:, tb, 8:9], eps_e[:, :], ALU.pow
                                        ).then_inc(rstd_ready, 1)

            def mid_tile(k, bk, o):
                if o == 0:
                    pool.wait_ge(filled, bk.filled(k, ("dn", TBB - 1)))
                pool.wait_ge(gate_up_ready, OT * k + (OT + o + 1))
                g = gus[o % 2]
                nc.gpsimd.tensor_tensor(gxu, g[:, 0, :], g[:, 1, :], ALU.mult).then_inc(gate_x_up, 1)
                pool.wait_ge(gate_x_up, OT * k + (o + 1))
                pool.wait_ge(sigmoid_ready, OT * k + (o + 1))
                nc.gpsimd.tensor_tensor(mid[:, o, :], gxu, th, ALU.mult).then_inc(mid_ready, 1)

            def chunk(k, turn):
                bk = Banks(turn)
                for q in range(QUADS):
                    if turn == "loop":
                        e, g = quad(q)
                        pr = q // QP
                        par = pr % 2
                        if q % QP == 0:
                            pool.wait_ge(tile_loaded[par], 32 * k + 16 * (pr // 2 + 1))
                            nc.gpsimd.tensor_tensor(dtu[par], tiles[par][:, :, 0, :], tiles[par][:, :, 1, :],
                                                    ALU.mult).then_inc(dtu_ready, 1)
                        if q < QP and q % 2 == 0:
                            pool.wait_ge(b_loaded[g], 16 * k + 16)
                        if q % QP == 0:
                            pool.wait_ge(dtu_ready, PAIRS * k + (pr + 1))
                        pool.wait_ge(scanned, QUADS * k + (QUADS + q - 1))
                        nc.gpsimd.tensor_tensor(
                            dbu[q % 2], dtu[par][:, e % 2, :].rearrange("p (a t) -> p a t", a=1).broadcast_to(
                                [P, QN, TB]), b_rep[:, QN * g:QN * g + QN, :], ALU.mult).then_inc(dbu_ready, 1)
                    for t in POOL_PLAN[q]:
                        if t[0] == "rstd":
                            rstd(k, t[1])
                        else:
                            mid_tile(k, bk, t[1])

            with pool.Fori(0, NB) as k:
                chunk(k, "loop")
            chunk(NB, "ffn")

        @block.tensor
        def _(pe):
            pe.wait_ge(s_const, 6)
            pe.wait_ge(v_tab, 18)
            for t, r in VT:
                for c in range(DK):
                    mm = nc.tensor.transpose(psum[:, 5 + t, r * c:r * c + r], tmp[0:r, t, P * c:P * c + P],
                                             ident[0:r, 0:r])
                mm.then_inc(t_tab, 1)
            pe.wait_ge(a_tab, 2 + 2 * DK)
            pe.wait_ge(s_in, 16)
            for t, r in VT:
                for e in range(4):
                    n = 4 * t + e
                    if n >= 4:
                        pe.wait_ge(a_tab, 2 + 2 * DK + n - 3)
                    for c in range(DK):
                        mm = nc.tensor.matmul(psum[0:r, e, :], xnt[:, c, P * t:P * t + r],
                                              inw[:, c, 512 * e:512 * e + 512], start=(c == 0), stop=(c == DK - 1))
                    mm.then_inc(t_tab, 1)

            def weight_tile(i, t):
                bank = p_w[t % 2]
                pe.wait_ge(ffw_ready, WPC * i + (t + 1))
                for v in range(LUTN):
                    pe.wait_ge(prod_ready, LUTN * WPC * i + (LUTN * (t + 1) + v + 1))
                    for c in range(DK):
                        mm = nc.tensor.matmul(bank[:, P * c:P * c + P], prod[v % 4][:, P * c:P * c + P], ident[:],
                                              is_transpose=True, start=(v == 0 and c == 0),
                                              stop=(v == LUTN - 1), skip_group_check=True)
                    mm.then_inc(prod_used, 1)

            def x_proj(i, e):
                pe.wait_ge(u_ready, ET * i + (e + 3))
                if e == 0:
                    pe.wait_ge(dtrow_ready, i + 1)
                nc.tensor.matmul(p_bc[0:2 * NS + 1, :], xpw[:, e, :], u_sb[:, e, :], start=(e == 0),
                                 stop=(e == ET - 1)).then_inc(xp_done, 1)

            pe.wait_ge(a_tab, 2 + 2 * DK + 8)
            pe.wait_ge(v_tab, 20)
            pe.wait_ge(s_pack, 96)
            pe.sem_inc(prod_used, 4)
            with pe.Fori(0, NA) as i:
                for e in range(ET):
                    if e == 0:
                        pe.wait_ge(oha_ready, 2 * i + 4)
                    pe.wait_ge(conv_done, ET * i + (e + 1))
                    cols = slice(P * e, P * e + P)
                    w = [xpart[:, m, cols] for m in range(3)] + [xpack[0:3 * V1, cols]]
                    for lo, n in ((0, TA), (TA, HALO)):
                        for m in range(4):
                            oh = oha[:, 0, lo:lo + n] if m < 3 else oha[0:3 * V1, 1, lo:lo + n]
                            mm = nc.tensor.matmul(pg[e % 2][:, lo:lo + n], w[m], oh, start=(m == 0), stop=(m == 3))
                    mm.then_inc(gathered, 1)
                    if e >= 2:
                        x_proj(i, e - 2)
                weight_tile(i, 0)
                x_proj(i, ET - 2)
                x_proj(i, ET - 1)
                weight_tile(i, 1)
                pe.wait_ge(dtrow_ready, i + 2)
                pe.wait_ge(relu_ready, ET * i + ET)
                nc.tensor.matmul(p_dt, pick[0:2 * NS + 1, :], bcs[0:2 * NS + 1, :], start=True, stop=True
                                 ).then_inc(dtrow_done, 1)
                for t in range(2, WPC):
                    weight_tile(i, t)
            weight_tile(NA, 0)

            pe.sem_inc(hc_used, QUADS)
            pe.sem_inc(filled, len(bank_uses(True, True)))

            def step(k, bk, t):
                name = t[0]
                use = t[:2]
                bank = shared[bk.bank(use)]
                if len(t) < 3 or t[2] == 0:
                    (who, n), back = bk.previous(use)
                    done, per, at = {"op": (h2_ready, TBB, n + 1), "xt": (xn2t_ready, TBB, n + 1),
                                     "gu": (gate_up_ready, OT, n + 1), "dn": (osb_ready, TBB, n + 1),
                                     "yb": (ysum_ready, 2 * PAIRS, 2 * n + 2), "sz": (yg_ready, PAIRS, n + 1)}[who]
                    pe.wait_ge(done, per * k + (per * (1 - back) + at))
                if name == "op":
                    tb, piece = t[1], t[2]
                    tt = slice(P * tb, P * tb + P)
                    if piece == 0:
                        pe.wait_ge(yg_ready, PAIRS * k + PAIRS) if tb == 0 else None
                        for m in range(4):
                            oh = ohb[:, 0, tt] if m < 3 else ohb[0:3 * V1, 1, tt]
                            w = part[:, m, CB:CB + DM] if m < 3 else pack[0:3 * V1, CB:CB + DM]
                            nc.tensor.matmul(bank, oh, w, start=(m == 0), stop=False)
                    for e in range(2 * piece, 2 * piece + 2):
                        mm = nc.tensor.matmul(bank, yg[:, e, tt], outw[:, e, :], start=False, stop=(e == ET - 1))
                elif name == "xt":
                    tb = t[1]
                    pe.wait_ge(xn2_ready, TBB * k + (TBB + tb + 1))
                    for c in range(DK):
                        mm = nc.tensor.matmul(bank[:, P * c:P * c + P], xn2[:, tb, P * c:P * c + P], ident[:],
                                              is_transpose=True, start=(c == 0), stop=(c == DK - 1),
                                              skip_group_check=True)
                elif name == "gu":
                    o, m = t[1], t[2]
                    if o == 0 and m == 0:
                        pe.wait_ge(xn2t_ready, TBB * k + 2 * TBB)
                    for c in range(DK):
                        mm = nc.tensor.matmul(bank[:, TB * m:TB * m + TB], ffw[:, OT * m + o, P * c:P * c + P],
                                              xn2t[:, c, :], start=(c == 0), stop=(c == DK - 1))
                elif name == "dn":
                    tb, piece = t[1], t[2]
                    if tb == 0 and piece == 0:
                        pe.wait_ge(mid_ready, OT * k + OT)
                    for o in range(2 * piece, min(2 * piece + 2, OT)):
                        mm = nc.tensor.matmul(bank, mid[:, o, P * tb:P * tb + P], ffw[:, 2 * OT + o, :],
                                              start=(o == 0), stop=(o == OT - 1))
                elif name == "sz":
                    pr = t[1] % PAIRS
                    if t[1] >= 0:
                        pe.wait_ge(ohb_ready, 2 * k + 4)
                    for e in range(2):
                        cols = slice(CZ + P * (2 * pr + e), CZ + P * (2 * pr + e + 1))
                        for m in range(4):
                            w = part[:, m, cols] if m < 3 else pack[0:3 * V1, cols]
                            oh = ohb[:, 0, :] if m < 3 else ohb[0:3 * V1, 1, :]
                            mm = nc.tensor.matmul(bank[:, TB * e:TB * e + TB], w, oh, start=(m == 0), stop=(m == 3))
                elif name == "yb":
                    pe.wait_ge(yts_ready, PAIRS * k + (PAIRS + t[1] + 1))
                    for e in range(2):
                        for b2 in range(TBB):
                            mm = nc.tensor.matmul(bank[:, TB * e + P * b2:TB * e + P * b2 + P],
                                                  yts[:, e, P * b2:P * b2 + P], ident[:], is_transpose=True,
                                                  start=(e == 0 and b2 == 0), stop=(e == 1 and b2 == TBB - 1),
                                                  skip_group_check=True)
                if name not in PARTS or t[2] == PARTS[name] - 1:
                    mm.then_inc(filled, 1)

            def chunk(k, turn):
                bk = Banks(turn)
                scan, ffn = turn == "loop", turn != "down"
                for q in range(QUADS):
                    if scan:
                        e, g = quad(q)
                        if q % QP == 0:
                            pe.wait_ge(yts_ready, PAIRS * k + (PAIRS + q // QP))
                        pe.wait_ge(hc_ready, QUADS * k + (QUADS + q + 1))
                        for i in range(QN):
                            for b2 in range(TBB):
                                mm = nc.tensor.matmul(p_yt[:, e % 2, b2, :], hc[q % NG][:, i, P * b2:P * b2 + P],
                                                      ident[:], is_transpose=True,
                                                      start=(q % QP == 0 and i == 0 and b2 == 0),
                                                      stop=(q % QP == QP - 1 and i == QN - 1 and b2 == TBB - 1),
                                                      skip_group_check=True)
                        mm.then_inc(hc_used, 1)
                    for t in PE_PLAN[q]:
                        if wanted(t, scan, ffn):
                            step(k, bk, t)

            pe.wait_ge(s_outw, 16)
            pe.wait_ge(ffw_ready, WTILES + 2)
            with pe.Fori(0, NB) as k:
                chunk(k, "loop")
            chunk(NB, "ffn")
            chunk(NB + 1, "down")

        @block.scalar
        def _(act):
            for n, (t, r) in enumerate(VT):
                act.wait_ge(v_tab, 4)
                nc.scalar.activation(tmp[0:r, t, :], tab[0:r, t, :], ACT.Exp, bias=stt[0:r, t, 1:2],
                                     accum_out=stt[0:r, t, 2:3]).then_inc(a_tab, 1)
            act.wait_ge(s_w, 16 * 9)
            for t, r in VT:
                act.wait_ge(t_tab, t + 1)
                for c in range(DK):
                    nc.scalar.activation(xnt[:, c, P * t:P * t + r], psum[:, 5 + t, r * c:r * c + r], ACT.Copy,
                                         scale=nw[:, c:c + 1]).then_inc(a_tab, 1)
            for t, r in VT:
                for e in range(4):
                    act.wait_ge(t_tab, 2 + 4 * t + e + 1)
                    if e < 2:
                        nc.scalar.activation(full[0:r, t, CX + 512 * e:CX + 512 * e + 512], psum[0:r, e, :],
                                             ACT.Copy).then_inc(a_tab, 1)
                    else:
                        nc.scalar.activation(full[0:r, t, CZ + 512 * (e - 2):CZ + 512 * (e - 1)], psum[0:r, e, :],
                                             ACT.Silu).then_inc(a_tab, 1)
            act.wait_ge(s_w, 16 * 9)
            nc.scalar.activation(a_neg[:], a_neg[:], ACT.Exp).then_inc(a_tab, 1)
            act.wait_ge(a_tab, 2 + 2 * DK + 8 + 1)
            nc.scalar.activation(a_neg[:], a_neg[:], ACT.Copy, scale=-1.0).then_inc(a_tab, 1)

            act.sem_inc(dtrow_ready, 1)
            act.sem_inc(relu_ready, ET)
            act.sem_inc(u_ready, 2)
            act.sem_inc(ffw_ready, 2)

            def silu(i, e):
                act.wait_ge(conv_done, ET * i + (e + 3))
                if e == 0:
                    act.wait_ge(u_stored, 16 * i + 16)
                nc.scalar.activation(u_sb[:, e, :], pre[e % 2], ACT.Silu).then_inc(u_ready, 1)

            def copy_weight_tile(i, t):
                act.wait_ge(prod_used, LUTN * WPC * i + (LUTN * (t + 1) + 4))
                dst = (ffw[:, WPC * i + t, :] if isinstance(i, int) else
                       ffw[:, bass.ds(WPC * i + t, 1), :].rearrange("p a c -> p (a c)"))
                nc.scalar.activation(dst, p_w[t % 2], ACT.Copy).then_inc(ffw_ready, 1)

            act.wait_ge(v_tab, 20)
            act.wait_ge(s_pack, 96)
            with act.Fori(0, NA) as i:
                for e in range(ET + 1):
                    if e < ET:
                        act.wait_ge(gathered, ET * i + e + 1)
                        act.wait_ge(conv_done, ET * i + (e + 1))
                        nc.scalar.activation(acc[e % 2], pg[e % 2][:, HALO:HALO + TA], ACT.Identity,
                                             scale=cw[:, e, 3:4], bias=cb[:, e:e + 1]).then_inc(acc_ready, 1)
                    if e >= 1:
                        silu(i, e - 1)
                act.wait_ge(u_ready, ET * i + (ET + 2))
                act.dma_start(chan[:, :, 1, bass.ds(TA * i, TA)], u_sb).then_inc(u_stored, 16)
                act.wait_ge(xp_done, ET * i + ET)
                act.wait_ge(bc_stored, 16 * i + 16)
                nc.scalar.activation(bcs[0:2 * NS + 1, :], p_bc[0:2 * NS + 1, :], ACT.Copy).then_inc(dtrow_ready, 1)
                act.wait_ge(dtrow_ready, i + 2)
                act.dma_start(bc[:, bass.ds(TA * i, TA)], bcs[0:2 * NS, :]).then_inc(bc_stored, 16)
                copy_weight_tile(i, 0)
                act.wait_ge(dtrow_done, i + 1)
                act.wait_ge(dt_stored, 16 * i + 16)
                for e in range(ET):
                    nc.scalar.activation(soft[:, e, :], p_dt, ACT.Abs, scale=dtw[:, e:e + 1],
                                         bias=dtb[:, e:e + 1]).then_inc(abs_done, 1)
                    nc.scalar.activation(relu[:, e, :], p_dt, ACT.Relu, scale=dtw[:, e:e + 1],
                                         bias=dtb[:, e:e + 1]).then_inc(relu_ready, 1)
                    if e == 5:
                        copy_weight_tile(i, 1)
                for h in range(2):
                    s4 = soft[:, 4 * h:4 * h + 4, :]
                    act.wait_ge(abs_done, ET * i + (4 * h + 4))
                    nc.scalar.activation(s4, s4, ACT.Exp, scale=-1.0).then_inc(exp_done, 1)
                copy_weight_tile(i, 2)
                for h in range(2):
                    s4 = soft[:, 4 * h:4 * h + 4, :]
                    act.wait_ge(exp_done, 2 * i + (h + 1))
                    nc.scalar.activation(s4, s4, ACT.Ln, bias=1.0).then_inc(soft_ready, 1)
                copy_weight_tile(i, 3)
            copy_weight_tile(NA, 0)

            act.sem_inc(saved, QUADS - 2)
            act.sem_inc(yts_ready, PAIRS - 1)
            act.sem_inc(h2_ready, TBB)
            act.sem_inc(kept, TBB)
            act.sem_inc(xn2t_ready, TBB)
            act.sem_inc(th_ready, OT)
            act.sem_inc(gate_up_ready, OT)
            for tb in range(TBB):
                act.sem_inc(out_stored[tb], 16)

            def save(k, q):
                e, g = quad(q % QUADS)
                n = NS * e + QN * g
                act.wait_ge(hc_ready, QUADS * k + (QUADS + q + 1))
                nc.scalar.activation(state[:, n:n + QN].rearrange("p (a b) -> p a b", b=1),
                                     hq[q % 2][:, :, TB - 1:TB], ACT.Copy).then_inc(saved, 1)
                act.wait_ge(saved, QUADS * k + (QUADS + q + 1))

            def step(k, bk, t):
                name = t[0]
                if name == "h2":
                    tb = t[1]
                    act.wait_ge(filled, bk.filled(k, ("op", tb)))
                    act.wait_ge(kept, TBB * k + (tb + 1))
                    nc.scalar.activation(h2[:, tb, :], shared[bk.bank(("op", tb))], ACT.Copy).then_inc(h2_ready, 1)
                elif name == "xnT":
                    tb = t[1]
                    act.wait_ge(filled, bk.filled(k, ("xt", tb)))
                    nc.scalar.activation(xn2t[:, :, P * tb:P * tb + P],
                                         shared[bk.bank(("xt", tb))].rearrange("p (c t) -> p c t", c=DK), ACT.Copy
                                         ).then_inc(xn2t_ready, 1)
                elif name == "tanh":
                    o = t[1]
                    bank = shared[bk.bank(("gu", o))]
                    act.wait_ge(filled, bk.filled(k, ("gu", o)))
                    act.wait_ge(mid_ready, OT * k + (OT + o))
                    nc.scalar.activation(th, bank[:, 0:TB], ACT.Tanh, scale=0.5).then_inc(th_ready, 1)
                    nc.scalar.activation(gus[o % 2].rearrange("p a t -> p (a t)"), bank, ACT.Copy
                                         ).then_inc(gate_up_ready, 1)
                    act.wait_ge(th_ready, OT * k + (OT + o + 1))
                    nc.scalar.activation(th, th, ACT.Copy, scale=0.5, bias=0.5).then_inc(sigmoid_ready, 1)
                elif name == "yT":
                    p = t[1]
                    act.wait_ge(hc_used, QUADS * k + (QUADS + QP * (p + 1)))
                    act.wait_ge(ysum_ready, 2 * PAIRS * k + (2 * PAIRS + 2 * p))
                    nc.scalar.activation(yts, p_yt.rearrange("p e b d -> p (e b d)").rearrange(
                        "p (e t) -> p e t", e=2), ACT.Copy).then_inc(yts_ready, 1)
                elif name == "store":
                    tb = t[1]
                    act.wait_ge(osb_ready, TBB * k + (TBB + tb + 1))
                    dst = (out[TB * k + P * tb:TB * k + P * tb + P, :] if isinstance(k, int) else
                           out[bass.ds(TB * k + P * tb, P), :])
                    act.dma_start(dst, osb[:, tb, :]).then_inc(out_stored[tb], 16)
                elif name == "keep":
                    tb = t[1]
                    act.wait_ge(out_stored[tb], 16 * k + 32)
                    nc.scalar.activation(osb[:, tb, :], h2[:, tb, :], ACT.Copy).then_inc(kept, 1)

            def chunk(k, turn):
                bk = Banks(turn)
                scan, ffn = turn == "loop", turn != "down"
                for q in range(QUADS):
                    if scan:
                        e, g = quad(q)
                        pr = q // QP
                        if q % QP == 0:
                            act.wait_ge(tile_loaded[pr % 2], 32 * k + 16 * (pr // 2 + 1))
                        save(k, q - 2)
                        for i in range(QN):
                            n = NS * e + QN * g + i
                            nc.scalar.activation(hq[q % 2][:, i, :], tiles[pr % 2][:, e % 2, 0, :], ACT.Exp,
                                                 scale=a_neg[:, n:n + 1]).then_inc(da_ready, 1)
                    for t in ACT_PLAN[q]:
                        if wanted(t, scan, ffn):
                            step(k, bk, t)

            act.wait_ge(b_start, 1)
            with act.Fori(0, NB) as k:
                chunk(k, "loop")
            chunk(NB, "ffn")
            chunk(NB + 1, "down")

        @block.vector
        def _(dve):
            dve.wait_ge(s_const, 6)
            nc.vector.tensor_copy(rows[:, 0:1], row_i[:, 0:1]).then_inc(v_tab, 1)
            dve.wait_ge(v_tab, 1)
            dve.wait_ge(s_tab, 32)
            nc.vector.tensor_scalar(rows[:, 1:2], rows[:, 0:1], float(V1), -float(V1), ALU.is_ge, ALU.mult
                                    ).then_inc(v_tab, 1)
            for t, r in VT:
                nc.vector.reduce_max(stt[0:r, t, 0:1], tab[0:r, t, :], AX_X)
                nc.vector.engine_nop() if False else None
            nc.vector.tensor_scalar(stt[:, 0, 15:16], rows[:, 0:1], 2.0 * V1, -float(V1), ALU.is_ge, ALU.mult
                                    ).then_inc(stats_part, 1)
            dve.wait_ge(stats_part, 1)
            dve.wait_ge(v_tab, 2)
            for n, (t, r) in enumerate(VT):
                nc.vector.tensor_scalar(stt[0:r, t, 1:2], stt[0:r, t, 0:1], -1.0, None, ALU.mult).then_inc(v_tab, 1)
            nc.vector.tensor_tensor(rows[:, 1:2], rows[:, 1:2], rows[:, 0:1], ALU.add).then_inc(stats_part, 1)
            dve.wait_ge(stats_part, 2)
            nc.vector.tensor_scalar(rows[:, 1:2], rows[:, 1:2], stt[:, 0, 15:16], float(P), ALU.add, ALU.add
                                    ).then_inc(stats_part, 1)
            for n, (t, r) in enumerate(VT):
                dve.wait_ge(a_tab, n + 1)
                nc.vector.reciprocal(stt[0:r, t, 3:4], stt[0:r, t, 2:3]).then_inc(v_tab, 1)
                dve.wait_ge(v_tab, 4 + 3 * n + 1)
                nc.vector.tensor_scalar(tab[0:r, t, :], tmp[0:r, t, :], stt[0:r, t, 3:4], None, ALU.mult
                                        ).then_inc(v_tab, 1)
                dve.wait_ge(v_tab, 4 + 3 * n + 2)
                nc.vector.bn_stats(rest[0:r, 8 * t:8 * t + 6], tab[0:r, t, :]).then_inc(stats_part, 1)
                dve.wait_ge(stats_part, 3 + n + 1)
                nc.vector.bn_aggr(stt[0:r, t, 7:9], rest[0:r, 8 * t:8 * t + 6]).then_inc(v_tab, 1)
            for n, (t, r) in enumerate(VT):
                dve.wait_ge(v_tab, 10)
                dve.wait_ge(g_tab, 2 * n + 2)
                nc.vector.tensor_scalar(tmp[0:r, t, :], tab[0:r, t, :], stt[0:r, t, 7:8], stt[0:r, t, 9:10],
                                        ALU.subtract, ALU.mult).then_inc(v_tab, 1)
                dve.wait_ge(v_tab, 10 + 3 * n + 1)
                nc.vector.tensor_tensor(full[0:r, t, CB:CB + DM], tab[0:r, t, :], tmp[0:r, t, :], ALU.add
                                        ).then_inc(v_tab, 1)
                dve.wait_ge(v_tab, 10 + 3 * n + 2)
                nc.vector.tensor_tensor_reduce(tab[0:r, t, :], tmp[0:r, t, :], tmp[0:r, t, :], 1.0, 0.0, ALU.mult,
                                               ALU.add, stt[0:r, t, 11:12]).then_inc(v_tab, 1)
            for n, (t, r) in enumerate(VT):
                dve.wait_ge(g_tab, 4 + 2 * n + 2)
                nc.vector.tensor_scalar(tmp[0:r, t, :], tmp[0:r, t, :], stt[0:r, t, 13:14], None, ALU.mult
                                        ).then_inc(v_tab, 1)
            dve.wait_ge(a_tab, 2 + 2 * DK + 8)
            chain = [5]

            def link(ins):
                chain[0] += 1
                ins.then_inc(stats_part, 1)
                dve.wait_ge(stats_part, chain[0])

            for t, r in VT:
                for lo, hi, dst in ((0, CX, part), (CX, CT, xpart)):
                    d3 = [(dst[:, m, :] if t == 0 else lo_st[0:r, m, lo:hi]) for m in range(3)]
                    src, rem = full[0:r, t, lo:hi], rest[0:r, lo:hi]
                    link(nc.vector.tensor_copy(d3[0], src))
                    link(nc.vector.tensor_tensor(rem, src, d3[0], ALU.subtract))
                    link(nc.vector.tensor_copy(d3[1], rem))
                    link(nc.vector.tensor_tensor(d3[2], rem, d3[1], ALU.subtract))
                nc.vector.tensor_copy(stt[0:r, t, 14:15], stt[0:r, t, 13:14]).then_inc(v_tab, 1)

            dve.wait_ge(s_pack, 96)
            dve.sem_inc(oha_ready, 2)
            dve.sem_inc(conv_done, 2)
            dve.sem_inc(prod_ready, LUTN)
            for s in (bc_stored, u_stored, dt_stored):
                dve.sem_inc(s, 16)

            def products(i, t):
                dve.wait_ge(widx_loaded[t % 2], 8 * WPC * i + 16 * (t // 2 + 1))
                for v in range(LUTN):
                    dve.wait_ge(prod_used, LUTN * WPC * i + (LUTN * t + v + 1))
                    nc.vector.tensor_scalar(prod[v % 4], widx_sb[t % 2], float(v), lut_sb[:, v:v + 1], ALU.is_equal,
                                            ALU.mult).then_inc(prod_ready, 1)

            with dve.Fori(0, NA) as i:
                dve.wait_ge(ids_loaded, 16 * i + 16)
                for m in range(2):
                    nc.vector.tensor_scalar(oha[:, m, 0:TA + HALO], idsa, rows[:, m:m + 1], None, ALU.is_equal
                                            ).then_inc(oha_ready, 1)
                for e in range(ET):
                    dve.wait_ge(acc_ready, ET * i + e + 1)
                    dve.wait_ge(u_ready, ET * i + (e + 1))
                    for m in (2, 1, 0):
                        src = acc[e % 2]
                        ins = nc.vector.scalar_tensor_tensor(
                            out=(pre[e % 2] if m == 0 else src), in0=pg[e % 2][:, m:m + TA], scalar=cw[:, e, m:m + 1],
                            in1=src, op0=ALU.mult, op1=ALU.add)
                        if m:
                            ins.then_inc(tap, 1)
                            dve.wait_ge(tap, 2 * ET * i + (2 * e + 3 - m))
                        else:
                            ins.then_inc(conv_done, 1)
                for t in range(WPC):
                    products(i, t)
            products(NA, 0)

            for s in (bc_stored, u_stored, dt_stored):
                dve.wait_ge(s, 16 * (NA + 1))
            dve.wait_ge(ffw_ready, WTILES + 2)
            taps = 2 * ET * NA
            for z in (yg, ohb, idsb, mid, osb, tiles[1], psum[:, 0:5, :]):
                taps += 1
                nc.vector.memset(z, 0 if z is idsb else 0.0).then_inc(tap, 1)
            dve.wait_ge(tap, taps)
            dve.sem_inc(scanned, QUADS)
            dve.sem_inc(hc_ready, QUADS)
            dve.sem_inc(yg_ready, PAIRS - 1)
            dve.sem_inc(ysum_ready, 2 * (PAIRS - 1))
            dve.sem_inc(ohb_ready, 2)
            dve.sem_inc(bn_part, TBB)
            dve.sem_inc(var_ready, TBB)
            dve.sem_inc(stats_ready, TBB)
            dve.sem_inc(xn2_ready, TBB)
            dve.sem_inc(osb_ready, TBB)
            dve.sem_inc(b_start, 1)

            def step(k, bk, t):
                name = t[0]
                if name == "stats":
                    tb = t[1]
                    dve.wait_ge(h2_ready, TBB * k + (TBB + tb + 1))
                    nc.vector.bn_stats(st2[:, tb, 0:6], h2[:, tb, :]).then_inc(bn_part, 1)
                    dve.wait_ge(s_const, 6)
                    dve.wait_ge(bn_part, TBB * k + (TBB + tb + 1))
                    nc.vector.bn_aggr(st2[:, tb, 6:8], st2[:, tb, 0:6]).then_inc(var_ready, 1)
                    dve.wait_ge(var_ready, TBB * k + (TBB + tb + 1))
                    nc.vector.tensor_scalar(st2[:, tb, 8:9], st2[:, tb, 7:8], EPS, None, ALU.add
                                            ).then_inc(stats_ready, 1)
                elif name == "norm":
                    tb = t[1]
                    dve.wait_ge(rstd_ready, TBB * k + (TBB + tb + 1))
                    nc.vector.tensor_scalar(xn2[:, tb, :], h2[:, tb, :], st2[:, tb, 6:7], st2[:, tb, 9:10],
                                            ALU.subtract, ALU.mult).then_inc(xn2_ready, 1)
                elif name == "onehot":
                    dve.wait_ge(idsb_loaded, 16 * k + 16)
                    dve.wait_ge(filled, bk.filled(k, ("op", TBB - 1)))
                    for m in range(2):
                        nc.vector.tensor_scalar(ohb[:, m, :], idsb, rows[:, m:m + 1], None, ALU.is_equal
                                                ).then_inc(ohb_ready, 1)
                elif name == "out":
                    tb = t[1]
                    b = bk.bank(("dn", tb))
                    dve.wait_ge(filled, bk.filled(k, ("dn", tb)))
                    dve.wait_ge(kept, TBB * k + (tb + 1))
                    nc.vector.tensor_tensor(osb[:, tb, :], osb[:, tb, :], shared[b], ALU.add).then_inc(osb_ready, 1)
                elif name == "fin":
                    p, pr = t[1], t[1] % PAIRS
                    b, bz = bk.bank(("yb", p)), bk.bank(("sz", p))
                    dve.wait_ge(filled, bk.filled(k, ("yb", p)))
                    for e in range(2):
                        nc.vector.scalar_tensor_tensor(
                            out=ysum[:, e, :], in0=tiles[pr % 2][:, e, 1, :], scalar=dpar[:, 2 * pr + e:2 * pr + e + 1],
                            in1=shared[b][:, TB * e:TB * e + TB], op0=ALU.mult, op1=ALU.add).then_inc(ysum_ready, 1)
                    dve.wait_ge(ysum_ready, 2 * PAIRS * k + (2 * PAIRS + 2 * p + 2))
                    nc.vector.tensor_tensor(yg[:, 2 * pr:2 * pr + 2, :], ysum,
                                            shared[bz].rearrange("p (e t) -> p e t", e=2), ALU.mult
                                            ).then_inc(yg_ready, 1)

            def chunk(k, turn):
                bk = Banks(turn)
                scan, ffn = turn == "loop", turn != "down"
                for q in range(QUADS):
                    if scan:
                        e, g = quad(q)
                        dve.wait_ge(dbu_ready, QUADS * k + (QUADS + q + 1))
                        dve.wait_ge(saved, QUADS * k + (q + 1))
                        for i in range(QN):
                            n = NS * e + QN * g + i
                            if i % 2 == 0:
                                dve.wait_ge(da_ready, NS * ET * k + (QN * q + i + 2))
                            h = hq[q % 2][:, i, :]
                            ins = nc.vector.tensor_tensor_scan(h, h, dbu[q % 2][:, i, :], state[:, n:n + 1],
                                                               ALU.mult, ALU.add)
                        ins.then_inc(scanned, 1)
                        if q < QP and q % 2 == 0:
                            dve.wait_ge(c_loaded[g], 16 * k + 16)
                        user = q - NG if q >= NG else max(u for u in range(QUADS) if u % NG == q % NG) - QUADS
                        dve.wait_ge(hc_used, QUADS * k + (QUADS + user + 1))
                        dve.wait_ge(scanned, QUADS * k + (QUADS + q + 1))
                        nc.vector.tensor_tensor(hc[q % NG], hq[q % 2], c_rep[:, QN * g:QN * g + QN, :], ALU.mult
                                                ).then_inc(hc_ready, 1)
                    for t in DVE_PLAN[q]:
                        if wanted(t, scan, ffn):
                            step(k, bk, t)

            with dve.Fori(0, NB // CPB) as s:
                dve.wait_ge(saved, NB // 2 * QUADS * s + QUADS)
                nc.vector.memset(state[:], 0.0).then_inc(state_clear, 1)
                with dve.Fori(0, CPB) as c:
                    dve.wait_ge(state_clear, s + 1)
                    chunk(s * CPB + c, "loop")
            chunk(NB, "ffn")
            chunk(NB + 1, "down")


def kernel(x, L0_tok_catid_time_matrix, L0_attn_norm_w, L0_attn_in_proj_w, L0_attn_conv_w, L0_attn_conv_b,
           L0_attn_x_proj_w, L0_attn_dt_w, L0_attn_dt_b, L0_attn_A_log, L0_attn_D_param, L0_attn_out_proj_w,
           L0_ffn_lut, L0_ffn_gate_idx, L0_ffn_up_idx, L0_ffn_down_idx):
    import numpy as np
    import concourse.bacc as bacc
    from concourse.bass_utils import run_bass_kernel_spmd

    def cols(v):
        v = np.asarray(v)
        return np.ascontiguousarray(v.reshape(-1, P).T)

    x = np.asarray(x)
    padded = np.pad(x, ((0, 0), (HALO, 0)), constant_values=-1)
    ids_a = np.stack([padded[b, TA * c:TA * c + TA + HALO] for b in range(2) for c in range(SEQ // TA)])
    pad = OT * P - FF
    gate = np.pad(np.asarray(L0_ffn_gate_idx), ((0, pad), (0, 0)), constant_values=-1).reshape(OT, P, DM)
    up = np.pad(np.asarray(L0_ffn_up_idx), ((0, pad), (0, 0)), constant_values=-1).reshape(OT, P, DM)
    down = np.pad(np.asarray(L0_ffn_down_idx), ((0, 0), (0, pad)), constant_values=-1)
    down = down.reshape(DK, P, OT, P).transpose(2, 1, 0, 3).reshape(OT, P, DM)
    arrays = {
        "ids_a": ids_a,
        "ids_b": x.reshape(NB, TB),
        "table": np.asarray(L0_tok_catid_time_matrix),
        "norm_w": cols(L0_attn_norm_w),
        "in_wT": np.asarray(L0_attn_in_proj_w).T,
        "conv_w": np.asarray(L0_attn_conv_w).reshape(ET, P, 4).transpose(1, 0, 2),
        "conv_b": cols(L0_attn_conv_b),
        "xp_wT": np.asarray(L0_attn_x_proj_w).T,
        "dt_w": cols(np.asarray(L0_attn_dt_w).reshape(-1)),
        "dt_b": cols(L0_attn_dt_b),
        "a_log": np.asarray(L0_attn_A_log).reshape(ET, P, NS).transpose(1, 0, 2).reshape(P, ET * NS),
        "d_par": cols(L0_attn_D_param),
        "out_wT": np.asarray(L0_attn_out_proj_w).T,
        "lut": np.asarray(L0_ffn_lut).reshape(1, LUTN),
        "widx": np.concatenate([gate, up, down]),
    }
    arrays = {n: np.ascontiguousarray(a) for n, a in arrays.items()}
    nc = bacc.Bacc("TRN2", target_bir_lowering=False, num_devices=1)
    args = [nc.dram_tensor(n, a.shape, mybir.dt.from_np(a.dtype), kind="ExternalInput").ap()
            for n, a in arrays.items()]
    out = nc.dram_tensor("out", (TOK + LAG * TB, DM), F32, kind="ExternalOutput").ap()
    lm_tower_kernel(nc, *args, out)
    r = run_bass_kernel_spmd(nc, [arrays], core_ids=[0])
    return np.asarray(r.results[0]["out"])[LAG * TB:].reshape(2, SEQ, DM)
```

```python
from contextlib import ExitStack

import concourse.bass as bass
from concourse import mybir

F32 = mybir.dt.float32
BF16 = mybir.dt.bfloat16
I32 = mybir.dt.int32
ALU = mybir.AluOpType
ACT = mybir.ActivationFunctionType
AX_X = mybir.AxisListType.X

P = 128
V = 168
V1 = V - P
DM = 512
DK = DM // P
DI = 1024
ET = DI // P
NS = 16
TOK = 4096
SEQ = 2048
LUTN = 16
FF = 1376
OT = (FF + P - 1) // P
WTILES = 3 * OT
EPS = 1e-5

TA = 512
HALO = 3
NA = TOK // TA
WPC = (WTILES - 1) // NA
TB = 256
NB = TOK // TB
CPB = SEQ // TB
TBB = TB // P
QN = 4
GQ = NS // QN
QUADS = ET * GQ
PAIRS = ET // 2
QP = 2 * GQ
NG = 3
ND = 3
SHARE = 2.93
FIRST_FREE = [-3, -1, -2]
GU0 = 15
NF = 3
LAG = 2

CB, CZ, CX = 0, DM, DM + DI
CT = DM + 2 * DI


def quad(q):
    return 2 * (q // QP) + q % 2, (q % QP) // 2


def last_user(q, n):
    return q - n if q >= n else max(u for u in range(QUADS) if u % n == q % n) - QUADS


def plan():
    pe, act, dve, pool = ({s: [] for s in range(QUADS)} for _ in range(4))
    for p in range(-1, PAIRS - 1):
        s = QP * p + QP
        act[s + 1] += [("yT", p)]
        act[s + QP - 2] += [("du", p + 1)]
        pe[s + QP - 2] += [("du", p + 1)]
        s = (1, 13, 21, 28)[p + 1]
        pe[s] += [("yb", p)]
        dve[s + 2] += [("fin", p)]
    for p, s in enumerate([9, 18, 23, 26]):
        pe[s] += [("sz", p)]
        act[s + 2] += [("szc", p)]
    for tb, s in enumerate([10, 12]):
        pe[s] += [("xt", tb)]

    pieces = [("op", 0, n) for n in range(6)] + [("gu", -1, n) for n in range(4)]
    pieces += [("op", 0, n) for n in (6, 7)] + [("op", 1, n) for n in range(8)]
    pieces += [("dn", tb, n) for tb in range(TBB) for n in range(OT)]
    pieces += [("gu", o, n) for o in range(OT - 1) for n in range(4)]
    small = {"sz": 1.0, "du": 0.5, "yb": 0.5, "xt": 0.5}
    last, room = {}, 0.0
    for s in range(QUADS):
        room += SHARE - sum(small[t[0]] for t in pe[s])
        while pieces and room > 0 and (pieces[0][:2] != ("gu", 0) or s >= GU0):
            t = pieces.pop(0)
            pe[s] += [t]
            last[t[:2]] = s
            room -= 1
        room = min(room, 0.5)
    assert not pieces

    for tb in range(TBB):
        s = last["op", tb]
        act[s + 2] += [("h2", tb)]
        dve[s + 3] += [("stats", tb)]
        pool[s + 5] += [("rstd", tb)]
        dve[s + 5] += [("norm", tb)]
        act[(10, 12)[tb] + 2] += [("xnT", tb)]
        s = last["dn", tb]
        dve[s + 2] += [("out", tb)]
        act[s + 4] += [("store", tb)]
        act[s + 10] += [("keep", tb)]
    dve[last["op", 1] + 1] += [("onehot",)]
    for o in range(-1, OT - 1):
        s = last["gu", o]
        if s + 2 < QUADS:
            act[s + 2] += [("tanh", o)]
            pool[min(s + 3, QUADS - 1)] += [("mid", o)]
        else:
            act[1].insert(0, ("tanh", o - OT))
            pool[3].insert(0, ("mid", o - OT))
    return pe, act, dve, pool


PE_PLAN, ACT_PLAN, DVE_PLAN, POOL_PLAN = plan()
PARTS = {"op": ET, "dn": OT, "gu": 4}


def wanted(t, scan, ffn):
    if t[0] in ("yb", "yT", "fin"):
        return scan or (ffn and t[1] < 0)
    if t[0] in ("onehot", "du", "sz", "szc"):
        return scan
    if t[0] in ("dn", "out", "store") or t[0] in ("gu", "tanh", "mid") and t[1] < 0:
        return True
    return ffn


def bank_uses(scan, ffn):
    seq = []
    for s in range(QUADS):
        for t in PE_PLAN[s]:
            if t[0] != "du" and wanted(t, scan, ffn) and t[:2] not in seq:
                seq.append(t[:2])
    return seq


def beside(e):
    return range(LUTN // ET * e, LUTN // ET * (e + 1))


def slot(plan, step):
    return [s for s in range(QUADS) if step in plan[s]][0]


def released(use):
    name, n = use
    step, plan = {"op": ("h2", ACT_PLAN), "xt": ("xnT", ACT_PLAN), "gu": ("tanh", ACT_PLAN), "dn": ("out", DVE_PLAN),
                  "yb": ("fin", DVE_PLAN), "sz": ("szc", ACT_PLAN)}[name]
    if name == "gu" and (step, n - OT) in sum(plan.values(), []):
        return QUADS + slot(plan, (step, n - OT))
    return slot(plan, (step, n))


class Banks:

    KINDS = {"loop": (True, True), "ffn": (False, True), "down": (False, False)}

    def __init__(self, turn):
        self.turn = turn
        self.seq, self.banks = self.assign(turn)
        self.turn_before = {"loop": "loop", "ffn": "loop", "down": "ffn"}[turn]
        self.before = self.assign(self.turn_before)
        self.done, self.done_before = self.finished(self.seq), self.finished(self.before[0])

    @staticmethod
    def finished(seq):
        return [t[:2] for s in range(QUADS) for t in PE_PLAN[s]
                if t[:2] in seq and (t[0] not in PARTS or t[2] == PARTS[t[0]] - 1)]

    def assign(self, turn):
        seq, banks, free = bank_uses(*self.KINDS[turn]), [], FIRST_FREE[:]
        for use in seq:
            b = free.index(min(free))
            banks.append(b)
            free[b] = released(use)
        return seq, banks

    def bank(self, use):
        if use not in self.seq:
            return self.before[1][self.before[0].index((use[0], use[1] + OT))]
        return self.banks[self.seq.index(use)]

    def filled(self, k, use):
        full = len(bank_uses(True, True))
        if use not in self.seq:
            return full * k + self.done_before.index((use[0], use[1] + OT)) + 1
        n = self.done.index(use) + 1
        if self.turn == "down":
            return full * k + len(self.before[0]) + n
        return full * k + (full + n)

    def previous(self, use):
        n = self.seq.index(use)
        b = self.banks[n]
        for m in range(n - 1, -1, -1):
            if self.banks[m] == b:
                return self.seq[m], 0
        seq, banks = self.before
        return [u for u, c in zip(seq, banks) if c == b][-1], 1


def lm_tower_kernel(nc, ids_a, ids_b, table, norm_w, in_wT, conv_w, conv_b, xp_wT, dt_w, dt_b, a_log,
                    d_par, out_wT, lut, widx, out):
    chan = nc.dram_tensor("chan", [P, ET, 2, TOK + TB], F32, kind="Internal").ap()
    bc = nc.dram_tensor("bc", [2 * NS, TOK], F32, kind="Internal").ap()

    with ExitStack() as ctx:
        def sb(name, shape, dt):
            return ctx.enter_context(nc.sbuf_tensor(name, shape, dt))

        def sem(name):
            return ctx.enter_context(nc.semaphore(name))

        ffw = sb("ffw", [P, WTILES, DM], F32)
        outw = sb("outw", [P, ET, DM], F32)
        part = sb("part", [P, 3, CX], BF16)
        pack = sb("pack", [P, CX], BF16)
        a_neg = sb("a_neg", [P, ET * NS], F32)
        dpar = sb("dpar", [P, ET], F32)
        ident = sb("ident", [P, P], F32)
        rows = sb("rows", [P, 2], F32)
        eps_e = sb("eps_e", [P, 1], F32)
        state = sb("state", [P, ET * NS], F32)
        work = sb("work", [P, 28720], F32)
        psum = ctx.enter_context(nc.psum_tensor("psum", [P, 8, 512], F32))

        class Region:

            def __init__(self, at=0):
                self.at = at

            def cut(self, shape, dt=F32):
                n = 1
                for d in shape:
                    n *= d
                words = (n * (2 if dt == BF16 else 4) + 3) // 4
                assert self.at + words <= 28720, self.at + words
                v = work[:, self.at:self.at + words]
                self.at += words
                if dt != F32:
                    v = v.bitcast(dt)
                    v = v[:, 0:n]
                if len(shape) == 2:
                    v = v.rearrange("p (a b) -> p a b", b=shape[1])
                elif len(shape) == 3:
                    v = v.rearrange("p (a b c) -> p a b c", b=shape[1], c=shape[2])
                return v

        ra = Region()
        u_sb = ra.cut([ET, TA])
        soft = ra.cut([ET, TA])
        relu = ra.cut([ET, TA])
        ra.at = 16384
        xpart = ra.cut([3, DI], BF16)
        xpack = ra.cut([DI], BF16)
        xpw = ra.cut([ET, 2 * NS + 1])
        pick = ra.cut([P])
        idsa = ra.cut([TA + HALO], I32)
        stage_a_buffers = ra.at
        oha = ra.cut([2, TA + HALO + 1], BF16)
        acc = [ra.cut([TA]) for _ in range(2)]
        pre = [ra.cut([TA]) for _ in range(2)]
        bcs = ra.cut([TA])
        widx_sb = [ra.cut([DM], I32) for _ in range(2)]
        prod = [ra.cut([DM]) for _ in range(4)]
        ra.at = max(ra.at, stage_a_buffers + 2 * DM + DK * V + 2 * DM + 3 * CT // 2 + 32)
        lut_sb = ra.cut([LUTN])
        cw = ra.cut([ET, 4])
        cb = ra.cut([ET])
        dtw = ra.cut([ET])
        dtb = ra.cut([ET])
        nw = ra.cut([DK])
        row_i = ra.cut([2], I32)
        rt = Region()
        inw = rt.cut([DK, 2 * DI])
        full = rt.cut([2, CT])
        rest = rt.cut([CT])
        rs2 = Region(stage_a_buffers)
        tab = rs2.cut([2, DM])
        xnt = rs2.cut([DK, V])
        tmp = rs2.cut([2, DM])
        lo_st = rs2.cut([3, CT], BF16)
        stt = rs2.cut([2, 16])

        rb = Region()
        b_rep = rb.cut([NS, TB])
        c_rep = rb.cut([NS, TB])
        tiles = [rb.cut([2, 2, TB]) for _ in range(2)]
        dtu = [rb.cut([2, TB]) for _ in range(2)]
        dbu = [rb.cut([QN, TB]) for _ in range(ND)]
        hc = [rb.cut([QN, TB]) for _ in range(NG)]
        yts = rb.cut([2, TBB * P])
        yg = rb.cut([ET, TB])
        h2 = rb.cut([TBB, DM])
        xn2 = rb.cut([TBB, DM])
        xn2t = rb.cut([DK, TB])
        mid = rb.cut([OT, TB])
        gus = [rb.cut([2, TB]) for _ in range(2)]
        th = rb.cut([TB])
        osb = rb.cut([TBB, DM])
        ohb = rb.cut([2, TB], BF16)
        idsb = rb.cut([TB], I32)
        st2 = rb.cut([TBB, 16])

        s_const = sem("constants_built")
        s_w = sem("small_weights_loaded")
        s_in = sem("in_proj_loaded")
        s_outw = sem("out_proj_loaded")
        s_tab = sem("table_loaded")
        v_tab = sem("table_steps_by_vector")
        a_tab = sem("table_steps_by_scalar")
        g_tab = sem("table_steps_by_pool")
        t_tab = sem("table_steps_by_tensor")
        s_pack = sem("pack_rows_moved")

        ids_loaded = sem("ids_loaded")
        oha_ready = sem("onehot_a_ready")
        gathered = sem("gathered")
        acc_ready = sem("acc_ready")
        tap = sem("conv_tap")
        conv_done = sem("conv_done")
        u_ready = sem("u_ready")
        xp_done = sem("x_proj_done")
        abs_done = sem("abs_done")
        relu_ready = sem("relu_ready")
        dtrow_ready = sem("dt_row_copied")
        dtrow_done = sem("dt_row_spread")
        exp_done = sem("exp_done")
        soft_ready = sem("soft_ready")
        dt_ready = sem("dt_ready")
        bc_stored = sem("bc_rows_stored")
        u_stored = sem("u_stored")
        dt_stored = sem("dt_stored")
        widx_loaded = [sem(f"weight_index_loaded{j}") for j in range(2)]
        prod_ready = sem("weight_product_ready")
        prod_used = sem("weight_product_used")
        ffw_ready = sem("weight_tile_copied")

        zeros_ready = sem("zeros_ready")
        cleared = sem("buffers_cleared")
        b_start = sem("stage_b_start")
        tile_loaded = [sem(f"tile_loaded{i}") for i in range(2)]
        b_loaded = [sem(f"b_loaded{g}") for g in range(GQ)]
        c_loaded = [sem(f"c_loaded{g}") for g in range(GQ)]
        idsb_loaded = sem("ids_b_loaded")
        state_clear = sem("state_cleared")
        da_ready = sem("decay_ready")
        dbu_ready = sem("dbu_ready")
        dtu_ready = sem("dtu_ready")
        du_ready = sem("skip_ready")
        silu_z_ready = sem("silu_z_copied")
        tile_used = sem("tile_used")
        pad_stored = sem("zeros_stored")
        scanned = sem("quad_scanned")
        hc_ready = sem("hc_ready")
        hc_used = sem("hc_used")
        saved = sem("state_saved")
        yts_ready = sem("y_time_major_copied")
        yg_ready = sem("y_gated_ready")
        ohb_ready = sem("onehot_b_ready")
        filled = sem("bank_filled")
        h2_ready = sem("h2_ready")
        stats_part = sem("ln_stats_part")
        stats_ready = sem("ln_stats_ready")
        bn_part = sem("ln_bn_stats_ready")
        var_ready = sem("ln_variance_ready")
        rstd_ready = sem("ln_rstd_ready")
        xn2_ready = sem("xn_ready")
        xn2t_ready = sem("xn_transposed")
        th_ready = sem("tanh_ready")
        gate_up_ready = sem("gate_up_copied")
        sigmoid_ready = sem("sigmoid_ready")
        gate_x_up = sem("gate_times_up_ready")
        mid_ready = sem("mid_ready")
        kept = sem("h2_kept")
        osb_ready = sem("out_tile_ready")
        out_stored = [sem(f"out_stored{tb}") for tb in range(TBB)]

        pg = [psum[:, 2 * i:2 * i + 2, :].rearrange("p a b -> p (a b)") for i in range(2)]
        p_bc, p_dt, p_w = psum[:, 4, :], psum[:, 5, :], [psum[:, 6, :], psum[:, 7, :]]
        hq = [psum[:, 2 * i:2 * i + 2, :].rearrange("p a b -> p (a b)").rearrange("p (i t) -> p i t", i=QN)
              for i in range(2)]
        p_yt = psum[:, 4, :].rearrange("p (e b d) -> p e b d", e=2, b=TBB)
        shared = [psum[:, 5 + b, :] for b in range(NF)]

        VT = ((0, P), (1, V1))

        block = ctx.enter_context(nc.Block())

        @block.sync
        def _(sp):
            sp.dma_start(tab[:, 0, :], table[0:P, :]).then_inc(s_tab, 16)
            sp.dma_start(tab[0:V1, 1, :], table[P:V, :]).then_inc(s_tab, 16)
            for dst, src in ((nw, norm_w), (cb, conv_b), (dtw, dt_w), (dtb, dt_b), (dpar[:], d_par),
                             (a_neg[:], a_log)):
                sp.dma_start(dst, src).then_inc(s_w, 16)
            sp.dma_start(cw, conv_w).then_inc(s_w, 16)
            sp.dma_start(xpw, xp_wT.rearrange("(e p) s -> p e s", p=P)).then_inc(s_w, 16)
            sp.dma_start(lut_sb, lut.broadcast_to([P, LUTN])).then_inc(s_w, 16)
            sp.dma_start(inw, in_wT.rearrange("(c p) e -> p c e", p=P)).then_inc(s_in, 16)
            sp.dma_start(outw[:], out_wT.rearrange("(e p) d -> p e d", p=P)).then_inc(s_outw, 16)
            sp.wait_ge(v_tab, 20)
            for j in range(3):
                sp.dma_start(pack[V1 * j:V1 * (j + 1), :], lo_st[0:V1, j, 0:CX]).then_inc(s_pack, 16)
                sp.dma_start(xpack[V1 * j:V1 * (j + 1), :], lo_st[0:V1, j, CX:CT]).then_inc(s_pack, 16)

            sp.wait_ge(s_pack, 96)
            sp.dma_start(widx_sb[0], widx[0]).then_inc(widx_loaded[0], 16)
            sp.dma_start(idsa, ids_a[0:1, :].broadcast_to([P, TA + HALO])).then_inc(ids_loaded, 16)
            with sp.Fori(0, NA) as i:
                sp.wait_ge(oha_ready, 2 * i + 4)
                sp.dma_start(idsa, ids_a[bass.ds(i + 1, 1), :].broadcast_to([P, TA + HALO])).then_inc(ids_loaded, 16)
                for t in range(WPC):
                    sp.wait_ge(prod_ready, LUTN * WPC * i + LUTN * (t + 1))
                    sp.dma_start(widx_sb[(t + 1) % 2], widx[bass.ds(WPC * i + (t + 1), 1), :, :].rearrange(
                        "a p c -> (a p) c")).then_inc(widx_loaded[(t + 1) % 2], 16)
                sp.wait_ge(dt_ready, 2 * i + 2)
                sp.dma_start(chan[:, :, 0, bass.ds(TA * i, TA)], relu).then_inc(dt_stored, 16)

            for s in (bc_stored, u_stored, dt_stored):
                sp.wait_ge(s, 16 * (NA + 1))
            sp.wait_ge(prod_ready, LUTN * (WTILES + 1))
            sp.wait_ge(ffw_ready, WTILES + 2)
            def load_tile(k, p):
                sp.wait_ge(tile_used, PAIRS * k + (PAIRS + p - 1))
                cols = slice(0, TB) if isinstance(k, int) else bass.ds(TB * k, TB)
                pr = p % PAIRS
                if p == PAIRS:
                    cols = bass.ds(TB * k + TB, TB)
                sp.dma_start(tiles[pr % 2].rearrange("p e a t -> p (e a) t"),
                             chan[:, 2 * pr:2 * pr + 2, :, cols].rearrange("p e a t -> p (e a) t")
                             ).then_inc(tile_loaded[pr % 2], 16)

            load_tile(0, 0)
            sp.wait_ge(b_start, 2)
            sp.dma_start(chan[:, 0:2, :, TOK:TOK + TB].rearrange("p e a t -> p (e a) t"),
                         osb.rearrange("p b (c t) -> p (b c) t", t=TB)).then_inc(pad_stored, 16)
            sp.wait_ge(pad_stored, 16)
            with sp.Fori(0, NB) as k:
                for g in range(GQ):
                    last = QUADS - QP + 2 * g + 2
                    sp.wait_ge(dbu_ready, QUADS * k + last)
                    sp.dma_start(b_rep[:, QN * g:QN * g + QN, :],
                                 bc[QN * g:QN * g + QN, bass.ds(TB * k, TB)].rearrange(
                                     "(a n) t -> a n t", a=1).broadcast_to([P, QN, TB])).then_inc(b_loaded[g], 16)
                    sp.wait_ge(hc_ready, QUADS * k + last)
                    sp.dma_start(c_rep[:, QN * g:QN * g + QN, :],
                                 bc[NS + QN * g:NS + QN * g + QN, bass.ds(TB * k, TB)].rearrange(
                                     "(a n) t -> a n t", a=1).broadcast_to([P, QN, TB])).then_inc(c_loaded[g], 16)
                load_tile(k, 1)
                sp.wait_ge(ohb_ready, 2 * k + 2)
                sp.dma_start(idsb, ids_b[bass.ds(k, 1), :].broadcast_to([P, TB])).then_inc(idsb_loaded, 16)
                for p in range(2, PAIRS + 1):
                    load_tile(k, p)
            for tb in range(TBB):
                sp.wait_ge(out_stored[tb], 16 * (NB + LAG + 1))

        @block.gpsimd
        def _(pool):
            nc.gpsimd.memset(ident[:], 0.0).then_inc(s_const, 1)
            nc.gpsimd.memset(eps_e[:], -0.5).then_inc(s_const, 1)
            nc.gpsimd.memset(pick[0:2 * NS, :], 0.0).then_inc(s_const, 1)
            nc.gpsimd.iota(row_i[:, 0:1], pattern=[[0, 1]], base=0, channel_multiplier=1).then_inc(s_const, 1)
            pool.wait_ge(s_const, 4)
            nc.gpsimd.memset(pick[2 * NS:2 * NS + 1, :], 1.0).then_inc(s_const, 1)
            pool.wait_ge(s_const, 5)
            nc.gpsimd.affine_select(out=ident[:], in_=ident[:], compare_op=ALU.not_equal, fill=1.0, base=0,
                                    pattern=[[-1, P]], channel_multiplier=1).then_inc(s_const, 1)
            for c in range(2):
                for n, (t, r) in enumerate(VT):
                    pool.wait_ge(v_tab, (10, 16)[c])
                    src = stt[0:r, t, (8, 11)[c]:(9, 12)[c]]
                    nc.gpsimd.tensor_scalar(stt[0:r, t, 12:13], src, (1.0, 1.0 / DM)[c], EPS, ALU.mult,
                                            ALU.add).then_inc(g_tab, 1)
                    pool.wait_ge(g_tab, 4 * c + 2 * n + 1)
                    nc.gpsimd.tensor_tensor(stt[0:r, t, (9, 13)[c]:(10, 14)[c]], stt[0:r, t, 12:13], eps_e[0:r, :],
                                            ALU.pow).then_inc(g_tab, 1)

            with pool.Fori(0, NA) as i:
                for h in range(2):
                    pool.wait_ge(soft_ready, 2 * i + (h + 1))
                    r4 = relu[:, 4 * h:4 * h + 4, :]
                    nc.gpsimd.tensor_tensor(r4, r4, soft[:, 4 * h:4 * h + 4, :], ALU.add).then_inc(dt_ready, 1)

            for s in (bc_stored, u_stored):
                pool.wait_ge(s, 16 * (NA + 1))
            pool.wait_ge(ids_loaded, 16 * (NA + 1))
            pool.wait_ge(ffw_ready, WTILES + 2)
            for z in (mid, osb, xn2t):
                nc.gpsimd.memset(z, 0.0).then_inc(zeros_ready, 1)
            pool.wait_ge(zeros_ready, 3)
            pool.sem_inc(b_start, 1)
            pool.wait_ge(b_start, 2)
            pool.sem_inc(dbu_ready, QUADS)
            pool.sem_inc(rstd_ready, TBB)
            pool.sem_inc(dtu_ready, PAIRS)
            pool.sem_inc(mid_ready, OT - 2)
            pool.sem_inc(gate_x_up, OT - 2)

            def rstd(k, tb):
                pool.wait_ge(stats_ready, TBB * k + (TBB + tb + 1))
                nc.gpsimd.tensor_tensor(st2[:, tb, 9:10], st2[:, tb, 8:9], eps_e[:, :], ALU.pow
                                        ).then_inc(rstd_ready, 1)

            def dt_times_u(k, pr):
                par = pr % 2
                pool.wait_ge(tile_loaded[par], 32 * k + 16 * (pr // 2 + 1))
                nc.gpsimd.tensor_tensor(dtu[par], tiles[par][:, :, 0, :], tiles[par][:, :, 1, :],
                                        ALU.mult).then_inc(dtu_ready, 1)

            def mid_tile(k, bk, o):
                if o == 0:
                    pool.wait_ge(filled, bk.filled(k, ("dn", TBB - 1)))
                pool.wait_ge(gate_up_ready, OT * k + (OT + o + 1))
                g = gus[o % OT % 2]
                nc.gpsimd.tensor_tensor(g[:, 0, :], g[:, 0, :], g[:, 1, :], ALU.mult).then_inc(gate_x_up, 1)
                pool.wait_ge(gate_x_up, OT * k + (OT + o + 1))
                pool.wait_ge(sigmoid_ready, OT * k + (OT + o + 1))
                nc.gpsimd.tensor_tensor(mid[:, o % OT, :], g[:, 0, :], th, ALU.mult).then_inc(mid_ready, 1)

            def chunk(k, turn):
                bk = Banks(turn)
                for q in range(QUADS):
                    if turn == "loop":
                        e, g = quad(q)
                        pr = q // QP
                        par = pr % 2
                        if q % QP == 5:
                            dt_times_u(k, pr + 1)
                        if q < QP and q % 2 == 0:
                            pool.wait_ge(b_loaded[g], 16 * k + 16)
                        if q % QP == 0:
                            pool.wait_ge(dtu_ready, PAIRS * k + (PAIRS + pr + 1))
                        pool.wait_ge(scanned, QUADS * k + (QUADS + last_user(q, ND) + 1))
                        nc.gpsimd.tensor_tensor(
                            dbu[q % ND], dtu[par][:, e % 2, :].rearrange("p (a t) -> p a t", a=1).broadcast_to(
                                [P, QN, TB]), b_rep[:, QN * g:QN * g + QN, :], ALU.mult).then_inc(dbu_ready, 1)
                    for t in POOL_PLAN[q]:
                        if t[0] == "rstd" and turn != "down":
                            rstd(k, t[1])
                        elif t[0] == "mid" and (turn != "down" or t[1] < 0):
                            mid_tile(k, bk, t[1])

            dt_times_u(0, 0)
            with pool.Fori(0, NB) as k:
                chunk(k, "loop")
            chunk(NB, "ffn")
            chunk(NB + 1, "down")

        @block.tensor
        def _(pe):
            pe.wait_ge(s_const, 6)
            pe.wait_ge(v_tab, 18)
            for t, r in VT:
                for c in range(DK):
                    mm = nc.tensor.transpose(psum[:, 5 + t, r * c:r * c + r], tmp[0:r, t, P * c:P * c + P],
                                             ident[0:r, 0:r])
                mm.then_inc(t_tab, 1)
            pe.wait_ge(a_tab, 2 + 2 * DK)
            pe.wait_ge(s_in, 16)
            for t, r in VT:
                for e in range(4):
                    n = 4 * t + e
                    if n >= 4:
                        pe.wait_ge(a_tab, 2 + 2 * DK + n - 3)
                    for c in range(DK):
                        mm = nc.tensor.matmul(psum[0:r, e, :], xnt[:, c, P * t:P * t + r],
                                              inw[:, c, 512 * e:512 * e + 512], start=(c == 0), stop=(c == DK - 1))
                    mm.then_inc(t_tab, 1)

            def weight_tile(i, t, vs=range(LUTN)):
                bank = p_w[t % 2]
                for v in vs:
                    if v == 0:
                        pe.wait_ge(ffw_ready, WPC * i + (t + 1))
                    pe.wait_ge(prod_ready, LUTN * WPC * i + (LUTN * (t + 1) + v + 1))
                    for c in range(DK):
                        mm = nc.tensor.matmul(bank[:, P * c:P * c + P], prod[v % 4][:, P * c:P * c + P], ident[:],
                                              is_transpose=True, start=(v == 0 and c == 0),
                                              stop=(v == LUTN - 1), skip_group_check=True)
                    mm.then_inc(prod_used, 1)

            def gather(i, e):
                if e == 0:
                    pe.wait_ge(oha_ready, 2 * i + 4)
                pe.wait_ge(conv_done, ET * i + (e + 1))
                cols = slice(P * e, P * e + P)
                w = [xpart[:, m, cols] for m in range(3)] + [xpack[0:3 * V1, cols]]
                for lo, n in ((0, TA), (TA, HALO)):
                    for m in range(4):
                        oh = oha[:, 0, lo:lo + n] if m < 3 else oha[0:3 * V1, 1, lo:lo + n]
                        mm = nc.tensor.matmul(pg[e % 2][:, lo:lo + n], w[m], oh, start=(m == 0), stop=(m == 3))
                mm.then_inc(gathered, 1)

            def x_proj(i, e):
                pe.wait_ge(u_ready, ET * i + (e + 3))
                if e == 0:
                    pe.wait_ge(dtrow_ready, i + 1)
                nc.tensor.matmul(p_bc[0:2 * NS + 1, :], xpw[:, e, :], u_sb[:, e, :], start=(e == 0),
                                 stop=(e == ET - 1)).then_inc(xp_done, 1)

            pe.wait_ge(a_tab, 2 + 2 * DK + 8)
            pe.wait_ge(v_tab, 20)
            pe.wait_ge(s_pack, 96)
            pe.sem_inc(prod_used, 4)
            gather(0, 0)
            gather(0, 1)
            with pe.Fori(0, NA) as i:
                for e in range(ET):
                    if e >= 2:
                        gather(i, e)
                        weight_tile(i, 0, beside(e - 2))
                        x_proj(i, e - 2)
                for e in (ET - 2, ET - 1):
                    weight_tile(i, 0, beside(e))
                    x_proj(i, e)
                weight_tile(i, 1, range(0, 4))
                pe.wait_ge(dtrow_ready, i + 2)
                pe.wait_ge(relu_ready, ET * i + ET)
                nc.tensor.matmul(p_dt, pick[0:2 * NS + 1, :], bcs[0:2 * NS + 1, :], start=True, stop=True
                                 ).then_inc(dtrow_done, 1)
                weight_tile(i, 1, range(4, LUTN))
                weight_tile(i, 2)
                gather(i + 1, 0)
                gather(i + 1, 1)
                weight_tile(i, 3)
            weight_tile(NA, 0)

            pe.sem_inc(hc_used, QUADS)
            pe.sem_inc(filled, len(bank_uses(True, True)))

            def skip(k, p):
                pe.wait_ge(du_ready, ET * k + (ET + 2 * p + 2))
                for e in range(2):
                    for b2 in range(TBB):
                        nc.tensor.matmul(p_yt[:, e, b2, :], yts[:, e, P * b2:P * b2 + P], ident[:], is_transpose=True,
                                         start=False, stop=False, skip_group_check=True)

            def step(k, bk, t):
                name = t[0]
                if name == "du":
                    skip(k, t[1])
                    return
                use = t[:2]
                bank = shared[bk.bank(use)]
                if len(t) < 3 or t[2] == 0:
                    (who, n), back = bk.previous(use)
                    done, per, at = {"op": (h2_ready, TBB, n + 1), "xt": (xn2t_ready, TBB, n + 1),
                                     "gu": (gate_up_ready, OT, n + 1), "dn": (osb_ready, TBB, n + 1),
                                     "yb": (yg_ready, PAIRS, n + 1),
                                     "sz": (silu_z_ready, PAIRS, n + 1)}[who]
                    pe.wait_ge(done, per * k + (per * (1 - back) + at))
                if name == "op":
                    tb, piece = t[1], t[2]
                    tt = slice(P * tb, P * tb + P)
                    if piece == 0:
                        for m in range(4):
                            oh = ohb[:, 0, tt] if m < 3 else ohb[0:3 * V1, 1, tt]
                            w = part[:, m, CB:CB + DM] if m < 3 else pack[0:3 * V1, CB:CB + DM]
                            nc.tensor.matmul(bank, oh, w, start=(m == 0), stop=False)
                    e = piece
                    if tb == 0 and e % 2 == 0:
                        pe.wait_ge(yg_ready, PAIRS * k + (e // 2 + 1))
                    mm = nc.tensor.matmul(bank, yg[:, e, tt], outw[:, e, :], start=False, stop=(e == ET - 1))
                elif name == "xt":
                    tb = t[1]
                    pe.wait_ge(xn2_ready, TBB * k + (TBB + tb + 1))
                    for c in range(DK):
                        mm = nc.tensor.matmul(bank[:, P * c:P * c + P], xn2[:, tb, P * c:P * c + P], ident[:],
                                              is_transpose=True, start=(c == 0), stop=(c == DK - 1),
                                              skip_group_check=True)
                elif name == "gu":
                    o, m = t[1], t[2] // 2
                    if o == 0 and t[2] == 0:
                        pe.wait_ge(xn2t_ready, TBB * k + 2 * TBB)
                    for c in range(DK // 2 * (t[2] % 2), DK // 2 * (t[2] % 2 + 1)):
                        mm = nc.tensor.matmul(bank[:, TB * m:TB * m + TB], ffw[:, OT * m + o % OT, P * c:P * c + P],
                                              xn2t[:, c, :], start=(c == 0), stop=(c == DK - 1))
                elif name == "dn":
                    tb, piece = t[1], t[2]
                    o = piece
                    if tb == 0:
                        pe.wait_ge(mid_ready, OT * k + (o + 1))
                    mm = nc.tensor.matmul(bank, mid[:, o, P * tb:P * tb + P], ffw[:, 2 * OT + o, :],
                                          start=(o == 0), stop=(o == OT - 1))
                elif name == "sz":
                    pr = t[1]
                    pe.wait_ge(ohb_ready, 2 * k + 4)
                    for e in range(2):
                        cols = slice(CZ + P * (2 * pr + e), CZ + P * (2 * pr + e + 1))
                        for m in range(4):
                            w = part[:, m, cols] if m < 3 else pack[0:3 * V1, cols]
                            oh = ohb[:, 0, :] if m < 3 else ohb[0:3 * V1, 1, :]
                            mm = nc.tensor.matmul(bank[:, TB * e:TB * e + TB], w, oh, start=(m == 0), stop=(m == 3))
                elif name == "yb":
                    pe.wait_ge(yts_ready, PAIRS * k + (PAIRS + t[1] + 1))
                    for e in range(2):
                        for b2 in range(TBB):
                            mm = nc.tensor.matmul(bank[:, TB * e + P * b2:TB * e + P * b2 + P],
                                                  yts[:, e, P * b2:P * b2 + P], ident[:], is_transpose=True,
                                                  start=(e == 0 and b2 == 0), stop=(e == 1 and b2 == TBB - 1),
                                                  skip_group_check=True)
                if name not in PARTS or t[2] == PARTS[name] - 1:
                    mm.then_inc(filled, 1)

            def chunk(k, turn):
                bk = Banks(turn)
                scan, ffn = turn == "loop", turn != "down"
                for q in range(QUADS):
                    if scan:
                        e, g = quad(q)
                        if q % QP == 0:
                            pe.wait_ge(yts_ready, PAIRS * k + (PAIRS + q // QP))
                        pe.wait_ge(hc_ready, QUADS * k + (QUADS + q + 1))
                        for i in range(QN):
                            for b2 in range(TBB):
                                mm = nc.tensor.matmul(p_yt[:, e % 2, b2, :], hc[q % NG][:, i, P * b2:P * b2 + P],
                                                      ident[:], is_transpose=True,
                                                      start=(q % QP == 0 and i == 0 and b2 == 0),
                                                      stop=(q % QP == QP - 1 and i == QN - 1 and b2 == TBB - 1),
                                                      skip_group_check=True)
                        mm.then_inc(hc_used, 1)
                    for t in PE_PLAN[q]:
                        if wanted(t, scan, ffn):
                            step(k, bk, t)

            pe.wait_ge(s_outw, 16)
            pe.wait_ge(ffw_ready, WTILES + 2)
            with pe.Fori(0, NB) as k:
                chunk(k, "loop")
            chunk(NB, "ffn")
            chunk(NB + 1, "down")

        @block.scalar
        def _(act):
            for n, (t, r) in enumerate(VT):
                act.wait_ge(v_tab, 4)
                nc.scalar.activation(tmp[0:r, t, :], tab[0:r, t, :], ACT.Exp, bias=stt[0:r, t, 1:2],
                                     accum_out=stt[0:r, t, 2:3]).then_inc(a_tab, 1)
            act.wait_ge(s_w, 16 * 9)
            for t, r in VT:
                act.wait_ge(t_tab, t + 1)
                for c in range(DK):
                    nc.scalar.activation(xnt[:, c, P * t:P * t + r], psum[:, 5 + t, r * c:r * c + r], ACT.Copy,
                                         scale=nw[:, c:c + 1]).then_inc(a_tab, 1)
            for t, r in VT:
                for e in range(4):
                    act.wait_ge(t_tab, 2 + 4 * t + e + 1)
                    if e < 2:
                        nc.scalar.activation(full[0:r, t, CX + 512 * e:CX + 512 * e + 512], psum[0:r, e, :],
                                             ACT.Copy).then_inc(a_tab, 1)
                    else:
                        nc.scalar.activation(full[0:r, t, CZ + 512 * (e - 2):CZ + 512 * (e - 1)], psum[0:r, e, :],
                                             ACT.Silu).then_inc(a_tab, 1)
            act.wait_ge(s_w, 16 * 9)
            nc.scalar.activation(a_neg[:], a_neg[:], ACT.Exp).then_inc(a_tab, 1)
            act.wait_ge(a_tab, 2 + 2 * DK + 8 + 1)
            nc.scalar.activation(a_neg[:], a_neg[:], ACT.Copy, scale=-1.0).then_inc(a_tab, 1)

            act.sem_inc(dtrow_ready, 1)
            act.sem_inc(relu_ready, ET)
            act.sem_inc(u_ready, 2)
            act.sem_inc(ffw_ready, 2)

            def silu(i, e):
                act.wait_ge(conv_done, ET * i + (e + 3))
                if e == 0:
                    act.wait_ge(u_stored, 16 * i + 16)
                nc.scalar.activation(u_sb[:, e, :], pre[e % 2], ACT.Silu).then_inc(u_ready, 1)

            def copy_weight_tile(i, t):
                act.wait_ge(prod_used, LUTN * WPC * i + (LUTN * (t + 1) + 4))
                dst = (ffw[:, WPC * i + t, :] if isinstance(i, int) else
                       ffw[:, bass.ds(WPC * i + t, 1), :].rearrange("p a c -> p (a c)"))
                nc.scalar.activation(dst, p_w[t % 2], ACT.Copy).then_inc(ffw_ready, 1)

            act.wait_ge(v_tab, 20)
            act.wait_ge(s_pack, 96)
            with act.Fori(0, NA) as i:
                for e in range(ET + 1):
                    if e < ET:
                        act.wait_ge(gathered, ET * i + e + 1)
                        act.wait_ge(conv_done, ET * i + (e + 1))
                        nc.scalar.activation(acc[e % 2], pg[e % 2][:, HALO:HALO + TA], ACT.Identity,
                                             scale=cw[:, e, 3:4], bias=cb[:, e:e + 1]).then_inc(acc_ready, 1)
                    if e >= 1:
                        silu(i, e - 1)
                act.wait_ge(u_ready, ET * i + (ET + 2))
                act.dma_start(chan[:, :, 1, bass.ds(TA * i, TA)], u_sb).then_inc(u_stored, 16)
                act.wait_ge(xp_done, ET * i + ET)
                act.wait_ge(bc_stored, 16 * i + 16)
                nc.scalar.activation(bcs[0:2 * NS + 1, :], p_bc[0:2 * NS + 1, :], ACT.Copy).then_inc(dtrow_ready, 1)
                act.wait_ge(dtrow_ready, i + 2)
                act.dma_start(bc[:, bass.ds(TA * i, TA)], bcs[0:2 * NS, :]).then_inc(bc_stored, 16)
                copy_weight_tile(i, 0)
                act.wait_ge(dtrow_done, i + 1)
                act.wait_ge(dt_stored, 16 * i + 16)
                for e in range(ET):
                    nc.scalar.activation(soft[:, e, :], p_dt, ACT.Abs, scale=dtw[:, e:e + 1],
                                         bias=dtb[:, e:e + 1]).then_inc(abs_done, 1)
                    nc.scalar.activation(relu[:, e, :], p_dt, ACT.Relu, scale=dtw[:, e:e + 1],
                                         bias=dtb[:, e:e + 1]).then_inc(relu_ready, 1)
                    if e == 4:
                        copy_weight_tile(i, 1)
                for h in range(2):
                    s4 = soft[:, 4 * h:4 * h + 4, :]
                    act.wait_ge(abs_done, ET * i + (4 * h + 4))
                    nc.scalar.activation(s4, s4, ACT.Exp, scale=-1.0).then_inc(exp_done, 1)
                copy_weight_tile(i, 2)
                for h in range(2):
                    s4 = soft[:, 4 * h:4 * h + 4, :]
                    act.wait_ge(exp_done, 2 * i + (h + 1))
                    nc.scalar.activation(s4, s4, ACT.Ln, bias=1.0).then_inc(soft_ready, 1)
                copy_weight_tile(i, 3)
            copy_weight_tile(NA, 0)

            act.sem_inc(saved, QUADS - 2)
            act.sem_inc(yts_ready, PAIRS - 1)
            act.sem_inc(da_ready, NS * ET)
            act.sem_inc(du_ready, ET)
            act.sem_inc(silu_z_ready, PAIRS)
            act.sem_inc(tile_used, PAIRS - 1)
            act.sem_inc(h2_ready, TBB)
            act.sem_inc(kept, TBB)
            act.sem_inc(xn2t_ready, TBB)
            act.sem_inc(th_ready, OT - 2)
            act.sem_inc(gate_up_ready, OT - 2)
            act.sem_inc(sigmoid_ready, OT - 2)
            for tb in range(TBB):
                act.sem_inc(out_stored[tb], 16)

            def save(k, q):
                e, g = quad(q % QUADS)
                n = NS * e + QN * g
                act.wait_ge(hc_ready, QUADS * k + (QUADS + q + 1))
                nc.scalar.activation(state[:, n:n + QN].rearrange("p (a b) -> p a b", b=1),
                                     hq[q % 2][:, :, TB - 1:TB], ACT.Copy).then_inc(saved, 1)
                act.wait_ge(saved, QUADS * k + (QUADS + q + 1))

            def step(k, bk, t):
                name = t[0]
                if name == "h2":
                    tb = t[1]
                    act.wait_ge(filled, bk.filled(k, ("op", tb)))
                    act.wait_ge(kept, TBB * k + (tb + 1))
                    nc.scalar.activation(h2[:, tb, :], shared[bk.bank(("op", tb))], ACT.Copy).then_inc(h2_ready, 1)
                elif name == "xnT":
                    tb = t[1]
                    act.wait_ge(filled, bk.filled(k, ("xt", tb)))
                    nc.scalar.activation(xn2t[:, :, P * tb:P * tb + P],
                                         shared[bk.bank(("xt", tb))].rearrange("p (c t) -> p c t", c=DK), ACT.Copy
                                         ).then_inc(xn2t_ready, 1)
                elif name == "tanh":
                    o = t[1]
                    bank = shared[bk.bank(("gu", o))]
                    act.wait_ge(filled, bk.filled(k, ("gu", o)))
                    act.wait_ge(mid_ready, OT * k + (OT + o))
                    nc.scalar.activation(th, bank[:, 0:TB], ACT.Tanh, scale=0.5).then_inc(th_ready, 1)
                    nc.scalar.activation(gus[o % OT % 2].rearrange("p a t -> p (a t)"), bank, ACT.Copy
                                         ).then_inc(gate_up_ready, 1)
                    act.wait_ge(th_ready, OT * k + (OT + o + 1))
                    nc.scalar.activation(th, th, ACT.Copy, scale=0.5, bias=0.5).then_inc(sigmoid_ready, 1)
                elif name == "yT":
                    p = t[1]
                    act.wait_ge(hc_used, QUADS * k + (QUADS + QP * (p + 1)))
                    nc.scalar.activation(yts, p_yt.rearrange("p e b d -> p (e b d)").rearrange(
                        "p (e t) -> p e t", e=2), ACT.Copy).then_inc(yts_ready, 1)
                elif name == "szc":
                    p = t[1]
                    act.wait_ge(filled, bk.filled(k, ("sz", p)))
                    nc.scalar.activation(yg[:, 2 * p:2 * p + 2, :].rearrange("p e t -> p (e t)"),
                                         shared[bk.bank(("sz", p))], ACT.Copy).then_inc(silu_z_ready, 1)
                elif name == "du":
                    p = t[1]
                    act.wait_ge(filled, bk.filled(k, ("yb", p - 1)))
                    for e in range(2):
                        nc.scalar.activation(yts[:, e, :], tiles[p % 2][:, e, 1, :], ACT.Copy,
                                             scale=dpar[:, 2 * p + e:2 * p + e + 1]).then_inc(du_ready, 1)
                elif name == "store":
                    tb = t[1]
                    act.wait_ge(osb_ready, TBB * k + (TBB + tb + 1))
                    dst = (out[TB * k + P * tb:TB * k + P * tb + P, :] if isinstance(k, int) else
                           out[bass.ds(TB * k + P * tb, P), :])
                    act.dma_start(dst, osb[:, tb, :]).then_inc(out_stored[tb], 16)
                elif name == "keep":
                    tb = t[1]
                    act.wait_ge(out_stored[tb], 16 * k + 32)
                    nc.scalar.activation(osb[:, tb, :], h2[:, tb, :], ACT.Copy).then_inc(kept, 1)

            def chunk(k, turn):
                bk = Banks(turn)
                scan, ffn = turn == "loop", turn != "down"
                for q in range(QUADS):
                    if scan:
                        e, g = quad(q)
                        pr = q // QP
                        if q % QP == 0:
                            act.wait_ge(tile_loaded[pr % 2], 32 * k + 16 * (pr // 2 + 1))
                        save(k, q - 2)
                        if q % QP == 1:
                            act.wait_ge(dtu_ready, PAIRS * k + (PAIRS + pr))
                            act.wait_ge(du_ready, ET * k + (ET + 2 * pr))
                            act.wait_ge(da_ready, NS * ET * k + (NS * ET + NS * 2 * pr))
                            act.sem_inc(tile_used, 1)
                        for i in range(QN):
                            n = NS * e + QN * g + i
                            nc.scalar.activation(hq[q % 2][:, i, :], tiles[pr % 2][:, e % 2, 0, :], ACT.Exp,
                                                 scale=a_neg[:, n:n + 1]).then_inc(da_ready, 1)
                    for t in ACT_PLAN[q]:
                        if wanted(t, scan, ffn):
                            step(k, bk, t)

            act.wait_ge(b_start, 2)
            with act.Fori(0, NB) as k:
                chunk(k, "loop")
            chunk(NB, "ffn")
            chunk(NB + 1, "down")

        @block.vector
        def _(dve):
            dve.wait_ge(s_const, 6)
            nc.vector.tensor_copy(rows[:, 0:1], row_i[:, 0:1]).then_inc(v_tab, 1)
            dve.wait_ge(v_tab, 1)
            dve.wait_ge(s_tab, 32)
            nc.vector.tensor_scalar(rows[:, 1:2], rows[:, 0:1], float(V1), -float(V1), ALU.is_ge, ALU.mult
                                    ).then_inc(v_tab, 1)
            for t, r in VT:
                nc.vector.reduce_max(stt[0:r, t, 0:1], tab[0:r, t, :], AX_X)
            nc.vector.tensor_scalar(stt[:, 0, 15:16], rows[:, 0:1], 2.0 * V1, -float(V1), ALU.is_ge, ALU.mult
                                    ).then_inc(stats_part, 1)
            dve.wait_ge(stats_part, 1)
            dve.wait_ge(v_tab, 2)
            for n, (t, r) in enumerate(VT):
                nc.vector.tensor_scalar(stt[0:r, t, 1:2], stt[0:r, t, 0:1], -1.0, None, ALU.mult).then_inc(v_tab, 1)
            nc.vector.tensor_tensor(rows[:, 1:2], rows[:, 1:2], rows[:, 0:1], ALU.add).then_inc(stats_part, 1)
            dve.wait_ge(stats_part, 2)
            nc.vector.tensor_scalar(rows[:, 1:2], rows[:, 1:2], stt[:, 0, 15:16], float(P), ALU.add, ALU.add
                                    ).then_inc(stats_part, 1)
            for n, (t, r) in enumerate(VT):
                dve.wait_ge(a_tab, n + 1)
                nc.vector.reciprocal(stt[0:r, t, 3:4], stt[0:r, t, 2:3]).then_inc(v_tab, 1)
                dve.wait_ge(v_tab, 4 + 3 * n + 1)
                nc.vector.tensor_scalar(tab[0:r, t, :], tmp[0:r, t, :], stt[0:r, t, 3:4], None, ALU.mult
                                        ).then_inc(v_tab, 1)
                dve.wait_ge(v_tab, 4 + 3 * n + 2)
                nc.vector.bn_stats(rest[0:r, 8 * t:8 * t + 6], tab[0:r, t, :]).then_inc(stats_part, 1)
                dve.wait_ge(stats_part, 3 + n + 1)
                nc.vector.bn_aggr(stt[0:r, t, 7:9], rest[0:r, 8 * t:8 * t + 6]).then_inc(v_tab, 1)
            for n, (t, r) in enumerate(VT):
                dve.wait_ge(v_tab, 10)
                dve.wait_ge(g_tab, 2 * n + 2)
                nc.vector.tensor_scalar(tmp[0:r, t, :], tab[0:r, t, :], stt[0:r, t, 7:8], stt[0:r, t, 9:10],
                                        ALU.subtract, ALU.mult).then_inc(v_tab, 1)
                dve.wait_ge(v_tab, 10 + 3 * n + 1)
                nc.vector.tensor_tensor(full[0:r, t, CB:CB + DM], tab[0:r, t, :], tmp[0:r, t, :], ALU.add
                                        ).then_inc(v_tab, 1)
                dve.wait_ge(v_tab, 10 + 3 * n + 2)
                nc.vector.tensor_tensor_reduce(tab[0:r, t, :], tmp[0:r, t, :], tmp[0:r, t, :], 1.0, 0.0, ALU.mult,
                                               ALU.add, stt[0:r, t, 11:12]).then_inc(v_tab, 1)
            for n, (t, r) in enumerate(VT):
                dve.wait_ge(g_tab, 4 + 2 * n + 2)
                nc.vector.tensor_scalar(tmp[0:r, t, :], tmp[0:r, t, :], stt[0:r, t, 13:14], None, ALU.mult
                                        ).then_inc(v_tab, 1)
            chain = [5]

            def link(ins):
                chain[0] += 1
                ins.then_inc(stats_part, 1)
                dve.wait_ge(stats_part, chain[0])

            for t, r in VT:
                dve.wait_ge(a_tab, 2 + 2 * DK + 4 * (t + 1))
                for lo, hi, dst in ((0, CX, part), (CX, CT, xpart)):
                    d3 = [(dst[:, m, :] if t == 0 else lo_st[0:r, m, lo:hi]) for m in range(3)]
                    src, rem = full[0:r, t, lo:hi], rest[0:r, lo:hi]
                    link(nc.vector.tensor_copy(d3[0], src))
                    link(nc.vector.tensor_tensor(rem, src, d3[0], ALU.subtract))
                    link(nc.vector.tensor_copy(d3[1], rem))
                    link(nc.vector.tensor_tensor(d3[2], rem, d3[1], ALU.subtract))
                nc.vector.tensor_copy(stt[0:r, t, 14:15], stt[0:r, t, 13:14]).then_inc(v_tab, 1)

            dve.wait_ge(s_pack, 96)
            dve.sem_inc(oha_ready, 2)
            dve.sem_inc(conv_done, 2)
            dve.sem_inc(prod_ready, LUTN)
            for s in (bc_stored, u_stored, dt_stored):
                dve.sem_inc(s, 16)

            def products(i, t, vs=range(LUTN)):
                for v in vs:
                    if v == 0:
                        dve.wait_ge(widx_loaded[t % 2], 8 * WPC * i + 16 * (t // 2 + 1))
                    dve.wait_ge(prod_used, LUTN * WPC * i + (LUTN * t + v + 1))
                    nc.vector.tensor_scalar(prod[v % 4], widx_sb[t % 2], float(v), lut_sb[:, v:v + 1], ALU.is_equal,
                                            ALU.mult).then_inc(prod_ready, 1)

            def onehots(i):
                dve.wait_ge(ids_loaded, 16 * i + 16)
                for m in range(2):
                    nc.vector.tensor_scalar(oha[:, m, 0:TA + HALO], idsa, rows[:, m:m + 1], None, ALU.is_equal
                                            ).then_inc(oha_ready, 1)

            onehots(0)
            with dve.Fori(0, NA) as i:
                for e in range(ET):
                    dve.wait_ge(acc_ready, ET * i + e + 1)
                    dve.wait_ge(u_ready, ET * i + (e + 1))
                    for m in (2, 1, 0):
                        src = acc[e % 2]
                        ins = nc.vector.scalar_tensor_tensor(
                            out=(pre[e % 2] if m == 0 else src), in0=pg[e % 2][:, m:m + TA], scalar=cw[:, e, m:m + 1],
                            in1=src, op0=ALU.mult, op1=ALU.add)
                        if m:
                            ins.then_inc(tap, 1)
                            products(i, 0, beside(e)[2 - m:3 - m])
                            dve.wait_ge(tap, 2 * ET * i + (2 * e + 3 - m))
                        else:
                            ins.then_inc(conv_done, 1)
                for t in range(1, WPC):
                    if t == 2:
                        onehots(i + 1)
                    products(i, t)
            products(NA, 0)

            for s in (bc_stored, u_stored):
                dve.wait_ge(s, 16 * (NA + 1))
            dve.wait_ge(ids_loaded, 16 * (NA + 1))
            dve.wait_ge(ffw_ready, WTILES + 2)
            for z in (yg, ohb, idsb, psum[:]):
                nc.vector.memset(z, 0 if z is idsb else 0.0).then_inc(cleared, 1)
            dve.wait_ge(cleared, 4)
            dve.sem_inc(scanned, QUADS)
            dve.sem_inc(hc_ready, QUADS)
            dve.sem_inc(yg_ready, PAIRS - 1)
            dve.sem_inc(ohb_ready, 2)
            dve.sem_inc(bn_part, TBB)
            dve.sem_inc(var_ready, TBB)
            dve.sem_inc(stats_ready, TBB)
            dve.sem_inc(xn2_ready, TBB)
            dve.sem_inc(osb_ready, TBB)
            dve.sem_inc(b_start, 1)

            def step(k, bk, t):
                name = t[0]
                if name == "stats":
                    tb = t[1]
                    dve.wait_ge(h2_ready, TBB * k + (TBB + tb + 1))
                    nc.vector.bn_stats(st2[:, tb, 0:6], h2[:, tb, :]).then_inc(bn_part, 1)
                    dve.wait_ge(s_const, 6)
                    dve.wait_ge(bn_part, TBB * k + (TBB + tb + 1))
                    nc.vector.bn_aggr(st2[:, tb, 6:8], st2[:, tb, 0:6]).then_inc(var_ready, 1)
                    dve.wait_ge(var_ready, TBB * k + (TBB + tb + 1))
                    nc.vector.tensor_scalar(st2[:, tb, 8:9], st2[:, tb, 7:8], EPS, None, ALU.add
                                            ).then_inc(stats_ready, 1)
                elif name == "norm":
                    tb = t[1]
                    dve.wait_ge(rstd_ready, TBB * k + (TBB + tb + 1))
                    nc.vector.tensor_scalar(xn2[:, tb, :], h2[:, tb, :], st2[:, tb, 6:7], st2[:, tb, 9:10],
                                            ALU.subtract, ALU.mult).then_inc(xn2_ready, 1)
                elif name == "onehot":
                    dve.wait_ge(idsb_loaded, 16 * k + 16)
                    dve.wait_ge(filled, bk.filled(k, ("op", TBB - 1)))
                    for m in range(2):
                        nc.vector.tensor_scalar(ohb[:, m, :], idsb, rows[:, m:m + 1], None, ALU.is_equal
                                                ).then_inc(ohb_ready, 1)
                elif name == "out":
                    tb = t[1]
                    b = bk.bank(("dn", tb))
                    dve.wait_ge(filled, bk.filled(k, ("dn", tb)))
                    dve.wait_ge(kept, TBB * k + (tb + 1))
                    nc.vector.tensor_tensor(osb[:, tb, :], osb[:, tb, :], shared[b], ALU.add).then_inc(osb_ready, 1)
                elif name == "fin":
                    p = t[1]
                    dve.wait_ge(filled, bk.filled(k, ("yb", p)))
                    dve.wait_ge(silu_z_ready, PAIRS * k + (PAIRS + p + 1))
                    y = yg[:, 2 * (p % PAIRS):2 * (p % PAIRS) + 2, :]
                    nc.vector.tensor_tensor(y, y, shared[bk.bank(("yb", p))].rearrange("p (e t) -> p e t", e=2),
                                            ALU.mult).then_inc(yg_ready, 1)

            def chunk(k, turn):
                bk = Banks(turn)
                scan, ffn = turn == "loop", turn != "down"
                for q in range(QUADS):
                    if scan:
                        e, g = quad(q)
                        dve.wait_ge(dbu_ready, QUADS * k + (QUADS + q + 1))
                        dve.wait_ge(saved, QUADS * k + (q + 1))
                        for i in range(QN):
                            n = NS * e + QN * g + i
                            if i % 2 == 0:
                                dve.wait_ge(da_ready, NS * ET * k + (NS * ET + QN * q + i + 2))
                            h = hq[q % 2][:, i, :]
                            ins = nc.vector.tensor_tensor_scan(h, h, dbu[q % ND][:, i, :], state[:, n:n + 1],
                                                               ALU.mult, ALU.add)
                        ins.then_inc(scanned, 1)
                        if q < QP and q % 2 == 0:
                            dve.wait_ge(c_loaded[g], 16 * k + 16)
                        dve.wait_ge(hc_used, QUADS * k + (QUADS + last_user(q, NG) + 1))
                        dve.wait_ge(scanned, QUADS * k + (QUADS + q + 1))
                        nc.vector.tensor_tensor(hc[q % NG], hq[q % 2], c_rep[:, QN * g:QN * g + QN, :], ALU.mult
                                                ).then_inc(hc_ready, 1)
                    for t in DVE_PLAN[q]:
                        if wanted(t, scan, ffn):
                            step(k, bk, t)

            with dve.Fori(0, NB // CPB) as s:
                dve.wait_ge(saved, NB // 2 * QUADS * s + QUADS)
                nc.vector.memset(state[:], 0.0).then_inc(state_clear, 1)
                with dve.Fori(0, CPB) as c:
                    dve.wait_ge(state_clear, s + 1)
                    chunk(s * CPB + c, "loop")
            chunk(NB, "ffn")
            chunk(NB + 1, "down")


def kernel(x, L0_tok_catid_time_matrix, L0_attn_norm_w, L0_attn_in_proj_w, L0_attn_conv_w, L0_attn_conv_b,
           L0_attn_x_proj_w, L0_attn_dt_w, L0_attn_dt_b, L0_attn_A_log, L0_attn_D_param, L0_attn_out_proj_w,
           L0_ffn_lut, L0_ffn_gate_idx, L0_ffn_up_idx, L0_ffn_down_idx):
    import numpy as np
    import concourse.bacc as bacc
    from concourse.bass_utils import run_bass_kernel_spmd

    def cols(v):
        v = np.asarray(v)
        return np.ascontiguousarray(v.reshape(-1, P).T)

    x = np.asarray(x)
    padded = np.pad(x, ((0, 0), (HALO, 0)), constant_values=-1)
    ids_a = np.stack([padded[b, TA * c:TA * c + TA + HALO] for b in range(2) for c in range(SEQ // TA)]
                     + [np.full(TA + HALO, -1, padded.dtype)])
    pad = OT * P - FF
    gate = np.pad(np.asarray(L0_ffn_gate_idx), ((0, pad), (0, 0)), constant_values=-1).reshape(OT, P, DM)
    up = np.pad(np.asarray(L0_ffn_up_idx), ((0, pad), (0, 0)), constant_values=-1).reshape(OT, P, DM)
    down = np.pad(np.asarray(L0_ffn_down_idx), ((0, 0), (0, pad)), constant_values=-1)
    down = down.reshape(DK, P, OT, P).transpose(2, 1, 0, 3).reshape(OT, P, DM)
    arrays = {
        "ids_a": ids_a,
        "ids_b": x.reshape(NB, TB),
        "table": np.asarray(L0_tok_catid_time_matrix),
        "norm_w": cols(L0_attn_norm_w),
        "in_wT": np.asarray(L0_attn_in_proj_w).T,
        "conv_w": np.asarray(L0_attn_conv_w).reshape(ET, P, 4).transpose(1, 0, 2),
        "conv_b": cols(L0_attn_conv_b),
        "xp_wT": np.asarray(L0_attn_x_proj_w).T,
        "dt_w": cols(np.asarray(L0_attn_dt_w).reshape(-1)),
        "dt_b": cols(L0_attn_dt_b),
        "a_log": np.asarray(L0_attn_A_log).reshape(ET, P, NS).transpose(1, 0, 2).reshape(P, ET * NS),
        "d_par": cols(L0_attn_D_param),
        "out_wT": np.asarray(L0_attn_out_proj_w).T,
        "lut": np.asarray(L0_ffn_lut).reshape(1, LUTN),
        "widx": np.concatenate([gate, up, down]),
    }
    arrays = {n: np.ascontiguousarray(a) for n, a in arrays.items()}
    nc = bacc.Bacc("TRN2", target_bir_lowering=False, num_devices=1)
    args = [nc.dram_tensor(n, a.shape, mybir.dt.from_np(a.dtype), kind="ExternalInput").ap()
            for n, a in arrays.items()]
    out = nc.dram_tensor("out", (TOK + LAG * TB, DM), F32, kind="ExternalOutput").ap()
    lm_tower_kernel(nc, *args, out)
    r = run_bass_kernel_spmd(nc, [arrays], core_ids=[0])
    return np.asarray(r.results[0]["out"])[LAG * TB:].reshape(2, SEQ, DM)
```
